# Optimizing a Trainium2 kernel written in Bass

```python
import numpy as np
import jax
import jax.numpy as jnp

def _softmax(x, axis=-1):
    return jax.nn.softmax(x, axis=axis)

def _gelu(x):
    return jax.nn.gelu(x, approximate=True)

def _silu(x):
    return jax.nn.silu(x)

def _sigmoid(x):
    return jax.nn.sigmoid(x)

def _layernorm(x, axis=-1, eps=1e-05):
    m = jnp.mean(x, axis=axis, keepdims=True)
    v = jnp.var(x, axis=axis, keepdims=True)
    return (x - m) / jnp.sqrt(v + eps)

def _scatter_add(tgt, idx, src, axis=0):
    return tgt.at[idx].add(src)

def _segment_sum(src, seg, n):
    return jax.ops.segment_sum(src, seg, n)
kernel_name = 'mk_prb_d1_jaxref_r4_89bd38'

def setup_inputs(seed: int=0):
    np.random.seed(seed)
    _w = jnp.asarray

    def _L0_attn_setup():
        import jax, jax.numpy as jnp
        import numpy as np
        D_MODEL = 256
        NUM_HEADS = 16
        D_K = D_MODEL // NUM_HEADS
        THETA = 10000.0
        NEG_INF = -1000000000.0

        def _rope(x, positions):
            half = D_K // 2
            inv_freq = 1.0 / THETA ** (jnp.arange(0, D_K, 2, dtype=jnp.float32) / D_K)
            angles = positions.astype(jnp.float32)[:, None] * inv_freq
            cos, sin = (jnp.cos(angles), jnp.sin(angles))
            xe = x[..., 0::2]
            xo = x[..., 1::2]
            re = xe * cos - xo * sin
            ro = xe * sin + xo * cos
            return jnp.stack([re, ro], axis=-1).reshape(x.shape).astype(x.dtype)
        key = jax.random.key(seed)
        ks = jax.random.split(key, 5)
        sigma = np.sqrt(2.0 / (D_MODEL + D_MODEL))
        x = jax.random.normal(ks[0], (2, 512, D_MODEL), dtype=jnp.float32)
        mk = lambda k: (sigma * jax.random.normal(k, (D_MODEL, D_MODEL))).astype(jnp.float32)
        return {'x': x, 'Wq': mk(ks[1]), 'bq': jnp.zeros((D_MODEL,), jnp.float32), 'Wk': mk(ks[2]), 'bk': jnp.zeros((D_MODEL,), jnp.float32), 'Wv': mk(ks[3]), 'bv': jnp.zeros((D_MODEL,), jnp.float32), 'Wo': mk(ks[4]), 'bo': jnp.zeros((D_MODEL,), jnp.float32), 'token_positions': jnp.arange(512, dtype=jnp.int64) if jax.config.jax_enable_x64 else jnp.arange(512, dtype=jnp.int32)}
    _L0_attn_in = _L0_attn_setup()

    def _L0_ffn_setup():
        import jax, jax.numpy as jnp
        import numpy as np
        DIM = 256

        def _reference_tuple_inner(x, W_r, W_k, W_v, mu_r, mu_k):
            B, T, C = x.shape
            x_prev = jnp.concatenate([jnp.zeros((B, 1, C), x.dtype), x[:, :-1, :]], axis=1)
            xr = mu_r * x + (1.0 - mu_r) * x_prev
            xk = mu_k * x + (1.0 - mu_k) * x_prev
            r = jax.nn.sigmoid(jnp.einsum('btc,dc->btd', xr, W_r))
            k = jnp.einsum('btc,dc->btd', xk, W_k)
            k_act = jnp.square(jax.nn.relu(k))
            out = r * jnp.einsum('btc,dc->btd', k_act, W_v)
            new_state = x[:, -1, :]
            return (out, new_state)
        key = jax.random.key(seed)
        ks = jax.random.split(key, 6)
        B, T, C = (8, 512, DIM)
        x = jax.random.normal(ks[0], (B, T, C), dtype=jnp.float32)
        s = 1.0 / np.sqrt(C)
        W_r = jax.random.uniform(ks[1], (C, C), jnp.float32, -s, s)
        W_k = jax.random.uniform(ks[2], (C, C), jnp.float32, -s, s)
        W_v = jax.random.uniform(ks[3], (C, C), jnp.float32, -s, s)
        mu_r = jax.random.uniform(ks[4], (C,), jnp.float32)
        mu_k = jax.random.uniform(ks[5], (C,), jnp.float32)
        return {'x': x, 'W_r': W_r, 'W_k': W_k, 'W_v': W_v, 'mu_r': mu_r, 'mu_k': mu_k}
    _L0_ffn_in = _L0_ffn_setup()
    _d = {'L0_attn_x': _L0_attn_in['x'], 'L0_attn_Wq': _L0_attn_in['Wq'], 'L0_attn_bq': _L0_attn_in['bq'], 'L0_attn_Wk': _L0_attn_in['Wk'], 'L0_attn_bk': _L0_attn_in['bk'], 'L0_attn_Wv': _L0_attn_in['Wv'], 'L0_attn_bv': _L0_attn_in['bv'], 'L0_attn_Wo': _L0_attn_in['Wo'], 'L0_attn_bo': _L0_attn_in['bo'], 'L0_attn_token_positions': _L0_attn_in['token_positions'], 'L0_ffn_W_r': _L0_ffn_in['W_r'], 'L0_ffn_W_k': _L0_ffn_in['W_k'], 'L0_ffn_W_v': _L0_ffn_in['W_v'], 'L0_ffn_mu_r': _L0_ffn_in['mu_r'], 'L0_ffn_mu_k': _L0_ffn_in['mu_k']}
    _x0 = _d['L0_attn_x']
    _d['L0_attn_x'] = jax.random.normal(jax.random.fold_in(jax.random.key(seed), 1), (32, 512, 256), dtype=_x0.dtype)
    del _x0
    return _d

def reference(L0_attn_x, L0_attn_Wq, L0_attn_bq, L0_attn_Wk, L0_attn_bk, L0_attn_Wv, L0_attn_bv, L0_attn_Wo, L0_attn_bo, L0_attn_token_positions, L0_ffn_W_r, L0_ffn_W_k, L0_ffn_W_v, L0_ffn_mu_r, L0_ffn_mu_k):

    def _L0_attn_ref(x, Wq, bq, Wk, bk, Wv, bv, Wo, bo, token_positions):
        import jax, jax.numpy as jnp
        import numpy as np
        D_MODEL = 256
        NUM_HEADS = 16
        D_K = D_MODEL // NUM_HEADS
        THETA = 10000.0
        NEG_INF = -1000000000.0

        def _rope(x, positions):
            half = D_K // 2
            inv_freq = 1.0 / THETA ** (jnp.arange(0, D_K, 2, dtype=jnp.float32) / D_K)
            angles = positions.astype(jnp.float32)[:, None] * inv_freq
            cos, sin = (jnp.cos(angles), jnp.sin(angles))
            xe = x[..., 0::2]
            xo = x[..., 1::2]
            re = xe * cos - xo * sin
            ro = xe * sin + xo * cos
            return jnp.stack([re, ro], axis=-1).reshape(x.shape).astype(x.dtype)
        B, S, D = x.shape
        Q = x @ Wq.T + bq
        K = x @ Wk.T + bk
        V = x @ Wv.T + bv

        def split_heads(t):
            return t.reshape(B, S, NUM_HEADS, D_K).transpose(0, 2, 1, 3)
        Q, K, V = (split_heads(Q), split_heads(K), split_heads(V))
        pos = jnp.arange(S)
        Q = _rope(Q, pos)
        K = _rope(K, pos)
        scale = 1.0 / jnp.sqrt(jnp.float32(D_K))
        scores = jnp.einsum('bhqd,bhkd->bhqk', Q, K) * scale
        causal = jnp.tril(jnp.ones((S, S), dtype=bool))
        scores = jnp.where(causal, scores, NEG_INF)
        weights = jax.nn.softmax(scores, axis=-1)
        attn = jnp.einsum('bhqk,bhkd->bhqd', weights, V)
        concat = attn.transpose(0, 2, 1, 3).reshape(B, S, D)
        return concat @ Wo.T + bo

    def _L0_ffn_ref(x, W_r, W_k, W_v, mu_r, mu_k):
        import jax, jax.numpy as jnp
        import numpy as np
        DIM = 256

        def _reference_tuple_inner(x, W_r, W_k, W_v, mu_r, mu_k):
            B, T, C = x.shape
            x_prev = jnp.concatenate([jnp.zeros((B, 1, C), x.dtype), x[:, :-1, :]], axis=1)
            xr = mu_r * x + (1.0 - mu_r) * x_prev
            xk = mu_k * x + (1.0 - mu_k) * x_prev
            r = jax.nn.sigmoid(jnp.einsum('btc,dc->btd', xr, W_r))
            k = jnp.einsum('btc,dc->btd', xk, W_k)
            k_act = jnp.square(jax.nn.relu(k))
            out = r * jnp.einsum('btc,dc->btd', k_act, W_v)
            new_state = x[:, -1, :]
            return (out, new_state)
        return _reference_tuple_inner(x, W_r, W_k, W_v, mu_r, mu_k)[0]
    x = L0_attn_x
    xn = _layernorm(x, axis=-1)
    x = x + _L0_attn_ref(xn, L0_attn_Wq, L0_attn_bq, L0_attn_Wk, L0_attn_bk, L0_attn_Wv, L0_attn_bv, L0_attn_Wo, L0_attn_bo, L0_attn_token_positions) + _L0_ffn_ref(xn, L0_ffn_W_r, L0_ffn_W_k, L0_ffn_W_v, L0_ffn_mu_r, L0_ffn_mu_k)
    return x

_drawn_inputs = setup_inputs


def setup_inputs(seed=0):
    import zlib

    import numpy as np

    out = dict(_drawn_inputs(seed))
    spreads = {'L0_attn_bq': (0.0, 0.602),
     'L0_attn_bk': (0.0, 0.8),
     'L0_attn_bv': (0.0, 0.1),
     'L0_attn_bo': (0.0, 0.1)}
    factors = {'L0_ffn_W_r': 3.246, 'L0_ffn_mu_r': 6.523}
    for name, (base, spread) in spreads.items():
        noise = np.random.default_rng([zlib.crc32(name.encode()), seed]).standard_normal(out[name].shape)
        drawn = base * np.exp(spread * noise) if base else spread * noise
        out[name] = jnp.asarray(drawn.astype(out[name].dtype))
    for name, factor in factors.items():
        out[name] = (out[name] * factor).astype(out[name].dtype)
    return out
```

```python
from contextlib import ExitStack

import numpy as np
import concourse.bass as bass
from concourse import mybir

F32 = mybir.dt.float32
F32R = mybir.dt.float32r
BF16 = mybir.dt.bfloat16
ALU = mybir.AluOpType
ACT = mybir.ActivationFunctionType

B, S, D = 32, 512, 256
H, DK = 16, 16
P = 128
TT = S // P
DC = D // P
GH = 4
NG = H // GH
STEPS = 16
SMAX_STEPS = 8
MROW = 64
ZROW = 80
GATHER = 16 * 8
KROWS = 96
EPS = 1e-5
NEG = -1e30

UNITS = [("T0", 0, 4), ("T1", 0, 5), ("QA", 0, 8), ("M0", 0, 9), ("QB", 0, 10),
         ("KA", 1, 1), ("KB", 1, 3), ("V0", 1, 5), ("V1", 1, 6), ("K0", 1, 8), ("M1", 1, 9), ("K1", 1, 10),
         ("O0", 2, 3), ("O1", 2, 5), ("R0", 2, 8), ("M2", 2, 9), ("R1", 2, 10),
         ("F0", 3, 3), ("F1", 3, 5), ("M3", 3, 9)]


def has(unit, b):
    if unit[0] == "M":
        return 0 <= 4 * b + int(unit[1]) + 1 < NG * B
    if unit[0] == "O":
        return b >= 1
    return b + 1 < B


def unit_count(b, unit):
    names = [u for u, _, _ in UNITS]
    if isinstance(b, int):
        before = sum(has(u, a) for a in range(-1, b) for u in names)
        return before + sum(has(u, b) for u in names[:names.index(unit) + 1])
    first = sum(has(u, a) for a in (-1, 0) for u in names)
    return b * len(names) + (first - len(names) + names.index(unit) + 1)


def ran(b):
    return not isinstance(b, int) or b >= -1


def past(count):
    return max(count, 0) if isinstance(count, int) else count


def layer_kernel(nc, x, wq, wk, wv, wo, wr, wf, wc, bq, bk, bv, bo, mu_r, mu_k, cos_t, sin_t, out):
    with ExitStack() as ctx:
        def sb(name, shape, dt=F32):
            return ctx.enter_context(nc.sbuf_tensor(name, shape, dt))

        def psum(name, shape):
            return ctx.enter_context(nc.psum_tensor(name, shape, F32))

        def sem(name):
            return ctx.enter_context(nc.semaphore(name))

        max_ps = psum("max_ps", [P, 2, S])
        exp_ps = psum("exp_ps", [P, 4, S])
        av_ps = psum("av_ps", [P, S])
        unit_ps = psum("unit_ps", [P, S])

        weights = {}
        for name in ("q", "k", "v", "o", "r", "f", "c"):
            weights[name] = [sb(f"w{name}_{part}", [P, DC, D], F32R) for part in ("hi", "lo")]
        cos_sb, sin_sb = sb("cos_sb", [P, S]), sb("sin_sb", [P, S])
        ident = sb("ident", [P, P])
        causal = sb("causal", [P, S], BF16)
        bias_q, bias_k = sb("bias_q", [P, 2]), sb("bias_k", [P, 2])
        mur_sb, muk_sb = sb("mur_sb", [P, DC]), sb("muk_sb", [P, DC])
        bv_sb, bo_sb = sb("bv_sb", [P, D]), sb("bo_sb", [P, D])
        minus_half = sb("minus_half", [P, TT])

        q_stack, k_stack = sb("q_stack", [KROWS, H, S], F32R), sb("k_stack", [KROWS, H, S], F32R)
        p_even = sb("p_even", [P, GH, S])
        p_odd = sb("p_odd", [P, GH, S - P])
        v_sb = [sb(f"v{i}", [P, TT * H // 2, 3, DK]) for i in range(2)]
        junk = sb("junk", [P, 2, S], BF16)
        mx = sb("mx", [P, P])
        negm_hi, negm_lo = sb("negm_hi", [GH * TT, P], F32R), sb("negm_lo", [GH * TT, P], F32R)
        av_sb = sb("av_sb", [P, 2, S])
        num = sb("num", [P, 2, S])
        sums, rsums = sb("sums", [P, 64]), sb("rsums", [P, 64])
        rec = sb("rec", [P, 2, S])
        rscratch = nc.dram_tensor("rscratch", (2, 2, GH, S), F32, kind="Internal").ap()

        x_in = sb("x_in", [P, TT, D])
        stats, mv = sb("stats", [P, TT, 6]), sb("mv", [P, TT, 2])
        veps, rstd = sb("veps", [P, TT]), sb("rstd", [P, TT])
        xnT = sb("xnT", [P, DC, S + 1])
        a_hi, a_lo = sb("a_hi", [P, DC, S], F32R), sb("a_lo", [P, DC, S], F32R)
        b_hi, b_lo = sb("b_hi", [P, DC, S], F32R), sb("b_lo", [P, DC, S], F32R)
        mix = sb("mix", [P, DC, S])
        act_sb = sb("act_sb", [P, DC * S])
        diff = act_sb[:, :].rearrange("p (c t) -> p c t", c=DC)
        relu_k = diff
        r_sb = act_sb[:, :].rearrange("p (a d) -> p a d", a=TT)
        rot = sb("rot", [P, 2, S])
        tmp = sb("tmp", [P, 2, S])
        q_parts, k_parts = sb("q_parts", [P, 2, 2, S], F32R), sb("k_parts", [P, 2, 2, S], F32R)
        y = [sb(f"y{i}", [P, TT, D]) for i in range(2)]

        w_in, c_in = sem("w_in"), sem("c_in")
        w_hi, w_lo, consts, zeroed, blank = (sem(n) for n in ("w_hi", "w_lo", "consts", "zeroed", "blank"))
        unit_full, unit_free = sem("unit_full"), sem("unit_free")
        max_full, max_done = sem("max_full"), sem("max_done")
        exp_full, exp_done = sem("exp_full"), sem("exp_done")
        masked, av_done, av_copied = sem("masked"), sem("av_done"), sem("av_copied")
        negm_ready, m_rows = sem("negm_ready"), sem("m_rows")
        q_loaded = [sem(f"q_loaded{i}") for i in range(2)]
        k_loaded = [sem(f"k_loaded{i}") for i in range(2)]
        gathered, recip_done, r_written, r_read = sem("gathered"), sem("recip_done"), sem("r_written"), sem("r_read")
        attn_ready, attn_hi, attn_lo = sem("attn_ready"), sem("attn_hi"), sem("attn_lo")
        stored = sem("stored")
        x_loaded, y_loaded, y_biased, y_ready = sem("x_loaded"), sem("y_loaded"), sem("y_biased"), sem("y_ready")
        ln_step, ln_stats, ln_rstd, xn_ready = sem("ln_step"), sem("ln_stats"), sem("ln_rstd"), sem("xn_ready")
        xn_hi, xn_lo, diff_ready = sem("xn_hi"), sem("xn_lo"), sem("diff_ready")
        mixed, mix_hi, mix_lo = sem("mixed"), sem("mix_hi"), sem("mix_lo")
        sin_done, rotated, rope_done, qk_hi, qk_lo = (sem(n) for n in ("sin_done", "rotated", "rope_done", "qk_hi", "qk_lo"))
        ksq, ksq_hi, ksq_lo, r_ready = sem("ksq"), sem("ksq_hi"), sem("ksq_lo"), sem("r_ready")

        sync_passed, vector_passed, gpsimd_passed = sem("sync_passed"), sem("vector_passed"), sem("gpsimd_passed")

        def p_of(kt):
            t = p_odd if kt % 2 else p_even
            return t[:, :, 0:S - P * kt]

        def program(eng, batch):
            batch(-1, 1)
            batch(0, 0)
            with eng.Fori(0, (B - 2) // 2) as i:
                batch(2 * i + 1, 1)
                batch(2 * i + 2, 0)
            batch(B - 1, 1)
            batch(B, 0)

        def flags(b):
            if isinstance(b, int):
                return 0 <= b < B, b + 1 < B, b >= 1
            return True, True, True

        def next_group(b, g):
            return not isinstance(b, int) or 0 <= NG * b + g + 1 < NG * B

        EXP_UNITS = [(0, 0, 2), (0, 2, 4), (1, 0, 2), (1, 2, 4), (2, 0, 4), (3, 0, 4)]
        EXP_STEP = [0, 2, 4, 6, 9, 12]
        LAST_UNIT = [2, 4, 5, 6]
        MASK_STEP = [3, 7, 10, 13]
        AV_STEP = [5, 9, 12]

        def exp_view(u):
            kt, h0, h1 = EXP_UNITS[u]
            banks = exp_ps[:, 2 * (u % 2):2 * (u % 2) + 2, :]
            if kt < 2:
                return banks[:, :, 0:S - P * kt]
            return banks.rearrange("p k (h t) -> p (k h) t", h=2)

        block = ctx.enter_context(nc.Block())

        @block.sync
        def _(sp):
            for n, (name, w) in enumerate((("q", wq), ("k", wk), ("v", wv), ("o", wo), ("r", wr), ("f", wf), ("c", wc))):
                raw = (p_even if n < 4 else p_odd)[:, :, :].rearrange("p h t -> p (h t)")
                sp.dma_start(raw[:, 512 * (n % 4):512 * (n % 4) + 512], w.rearrange("p c d -> p (c d)")).then_inc(w_in, 16)
            for dst, src in ((cos_sb, cos_t), (sin_sb, sin_t), (bias_q, bq), (bias_k, bk), (mur_sb, mu_r), (muk_sb, mu_k)):
                sp.dma_start(dst[:, :], src).then_inc(c_in, 16)
            for dst, src in ((bv_sb, bv), (bo_sb, bo)):
                sp.dma_start(dst[:, :], src.unsqueeze(0).to_broadcast([P, D])).then_inc(c_in, 16)
            sp.wait_ge(zeroed, 6)

            def stack_rows(stack, row, rows, head, heads):
                return stack[row:row + rows, head:head + heads, :].rearrange("r h t -> r (h t)").bitcast(F32)

            def load_stack(stack, parts, order, half, loaded):
                for term, part in enumerate(order):
                    for ab in range(2):
                        row = 16 * term + 8 * ab
                        sp.dma_start(stack_rows(stack, row, 8, 8 * half, 8),
                                     parts[64 * half:64 * half + 64, part, ab, :].bitcast(F32)).then_inc(loaded, 16)

            def load_queries(n, half):
                sp.wait_ge(qk_hi, 2 * n + 1)
                sp.sem_inc(sync_passed, 1)
                sp.wait_ge(qk_lo, 2 * n + 1)
                sp.sem_inc(sync_passed, 1)
                load_stack(q_stack, q_parts, (0, 1, 0), half, q_loaded[half])
                sp.dma_start(stack_rows(q_stack, MROW, 2, 8 * half, 8), stack_rows(q_stack, ZROW, 2, 8 * half, 8)).then_inc(q_loaded[half], 16)

            def load_keys(n, half):
                sp.wait_ge(qk_hi, 2 * n + 2)
                sp.sem_inc(sync_passed, 1)
                sp.wait_ge(qk_lo, 2 * n + 2)
                sp.sem_inc(sync_passed, 1)
                load_stack(k_stack, k_parts, (0, 0, 1), half, k_loaded[half])

            def gather(b, q):
                pair = 2 * b + q
                sp.wait_ge(av_copied, 2 * (pair + 1))
                sp.sem_inc(sync_passed, 1)
                sp.wait_ge(attn_ready, past(b))
                sp.sem_inc(sync_passed, 1)
                sp.wait_ge(recip_done, past(pair - 1))
                sp.sem_inc(sync_passed, 1)
                for j in range(GH):
                    src = 32 * j + 16 * (j % 2)
                    sp.dma_start(num[64 * q + 16 * j:64 * q + 16 * j + 16, :, :],
                                 av_sb[src:src + 16, :, :]).then_inc(gathered, 16)
                for par in range(2):
                    for j in (0, 2):
                        dst, src = 64 * q + 32 * par + 8 * j, 32 * j + 16
                        sp.dma_start(sums[dst:dst + 16, :], av_sb[src:src + 17:16, par, :]).then_inc(gathered, 16)

            def spread(b, q):
                pair = 2 * b + q
                sp.wait_ge(recip_done, pair + 1)
                sp.sem_inc(sync_passed, 1)
                sp.wait_ge(r_read, past(32 * (pair - 1)))
                sp.sem_inc(sync_passed, 1)
                sp.wait_ge(attn_ready, past(b))
                sp.dma_start(rscratch[q].rearrange("g h (a t) -> (g h a) t", a=8), rsums[64 * q:64 * q + 64, :]).then_inc(r_written, 16)
                sp.wait_ge(r_written, 16 * (pair + 1))
                sp.sem_inc(sync_passed, 1)
                for par in range(2):
                    sp.dma_start(rec[64 * q:64 * q + 64, par, :],
                                 rscratch[q, par].unsqueeze(1).to_broadcast([GH, DK, S])).then_inc(r_read, 16)

            def batch(b, par):
                attends, front, prev = flags(b)
                n, ypar = b + 1, 1 - par
                for g in range(NG):
                    for s in range(STEPS):
                        if (g, s) == (0, 0) and front:
                            if ran(b - 1):
                                sp.wait_ge(unit_full, unit_count(b - 1, "R1"))
                            sp.dma_start(x_in[:, :, :], row(x_tiles, n)).then_inc(x_loaded, 16)
                        if (g, s) == (0, 2) and prev:
                            gather(b - 1, 1)
                        if (g, s) == (0, 3) and attends:
                            sp.wait_ge(exp_full, past(24 * b))
                            sp.sem_inc(sync_passed, 1)
                            load_queries(b, 1)
                            load_keys(b, 1)
                        if (g, s) == (2, 2) and attends:
                            gather(b, 0)
                        if (g, s) == (2, 2) and front:
                            sp.wait_ge(exp_full, past(24 * b + 12))
                            sp.sem_inc(sync_passed, 1)
                            load_queries(n, 0)
                            load_keys(n, 0)
                        if (g, s) == (2, 6) and prev:
                            sp.wait_ge(unit_free, unit_count(b, "O1"))
                            sp.dma_start(row(out_tiles, b - 1), y[ypar][:, :, :]).then_inc(stored, 16)
                        if (g, s) == (2, 12) and front:
                            sp.wait_ge(stored, past(16 * (b if prev else 0)))
                            sp.dma_start(y[ypar][:, :, :], row(x_tiles, n)).then_inc(y_loaded, 16)
                        if s == 9 and next_group(b, g):
                            nxt = NG * b + g + 1
                            sp.wait_ge(unit_free, unit_count(b, f"M{g}"))
                            sp.sem_inc(sync_passed, 1)
                            h0 = (GH * (g + 1)) % H
                            for r, part in enumerate((negm_hi, negm_lo)):
                                sp.dma_start(stack_rows(q_stack, MROW + r, 1, h0, GH), part[:, :].bitcast(F32)).then_inc(m_rows, 16)
                        if (g, s) == (0, 10) and prev:
                            spread(b - 1, 1)
                        if (g, s) == (2, 9) and attends:
                            spread(b, 0)

            x_tiles = x.rearrange("b (a p) d -> b p a d", p=P)
            out_tiles = out.rearrange("b (a p) d -> b p a d", p=P)

            def row(ap, b):
                return ap[b] if isinstance(b, int) else ap[bass.ds(b, 1)].rearrange("o p a d -> p (o a) d")

            program(sp, batch)
            sp.wait_ge(stored, 16 * B)

        @block.tensor
        def _(pe):
            pe.wait_ge(consts, 4)
            pe.wait_ge(zeroed, 6)
            pe.wait_ge(w_hi, 7)
            pe.wait_ge(w_lo, 7)

            def claim(b, unit):
                pe.wait_ge(unit_free, past(unit_count(b, unit) - 1))

            def project(hi_lo, w, token_tiles=None, cols=None):
                terms = [(c, i, j) for c in range(DC) for i, j in ((0, 0), (0, 1), (1, 0))]
                if token_tiles is None:
                    for m, (c, i, j) in enumerate(terms):
                        last = nc.tensor.matmul(unit_ps[:, :], weights[w][j][:, c, cols:cols + P], hi_lo[i][:, c, :],
                                                start=m == 0, stop=m == 5)
                else:
                    for k, a in enumerate(token_tiles):
                        for m, (c, i, j) in enumerate(terms):
                            last = nc.tensor.matmul(unit_ps[:, D * k:D * k + D], hi_lo[i][:, c, P * a:P * a + P],
                                                    weights[w][j][:, c, :], start=m == 0, stop=m == 5)
                last.then_inc(unit_full, 1)

            def unit(b, name):
                claim(b, name)
                n, kind, k = b + 1, name[0], name[1:]
                if kind == "T":
                    pe.wait_ge(xn_ready, n + 1)
                    for a in range(TT):
                        last = nc.tensor.transpose(unit_ps[:, P * a:P * a + P], x_in[:, a, P * int(k):P * int(k) + P], ident[:, :])
                    last.then_inc(unit_full, 1)
                elif name in ("QA", "QB", "KA", "KB"):
                    if name == "QA":
                        pe.wait_ge(xn_hi, n + 1)
                        pe.wait_ge(xn_lo, n + 1)
                    project((a_hi, a_lo), kind.lower(), cols=P * "AB".index(k))
                elif kind == "V":
                    project((a_hi, a_lo), "v", token_tiles=(2 * int(k), 2 * int(k) + 1))
                elif kind == "K":
                    pe.wait_ge(mix_hi, 2 * n + 1)
                    pe.wait_ge(mix_lo, 2 * n + 1)
                    project((b_hi, b_lo), "f", cols=P * int(k))
                elif kind == "R":
                    pe.wait_ge(mix_hi, 2 * n + 2)
                    pe.wait_ge(mix_lo, 2 * n + 2)
                    project((b_hi, b_lo), "r", token_tiles=(2 * int(k), 2 * int(k) + 1))
                elif kind == "F":
                    pe.wait_ge(ksq_hi, n + 1)
                    pe.wait_ge(ksq_lo, n + 1)
                    project((a_hi, a_lo), "c", token_tiles=(2 * int(k), 2 * int(k) + 1))
                elif kind == "O":
                    pe.wait_ge(attn_hi, b)
                    pe.wait_ge(attn_lo, b)
                    project((a_hi, a_lo), "o", token_tiles=(2 * int(k), 2 * int(k) + 1))
                elif kind == "M":
                    pe.wait_ge(max_done, 16 * (NG * b + int(k) + 2))
                    nc.tensor.transpose(unit_ps[:, 0:P], mx[:, :], ident[:, :]).then_inc(unit_full, 1)

            def max_scores(b, g, u):
                nxt = 16 * (NG * b + g + 1) + u
                h, qt = (GH * (g + 1)) % H + u // TT, u % TT
                if u == 0:
                    half = h // 8
                    nb = b + 1 if g == NG - 1 else b
                    pe.wait_ge(q_loaded[half], 112 * (nb + 1))
                    pe.wait_ge(k_loaded[half], 96 * (nb + 1))
                pe.wait_ge(max_done, past(nxt - 1))
                keys = max(2 * P, P * (qt + 1))
                nc.tensor.matmul(max_ps[:, u % 2, 0:keys], q_stack[:, h, P * qt:P * qt + P], k_stack[:, h, 0:keys],
                                 start=True, stop=True).then_inc(max_full, 1)

            def exp_scores(b, g, u):
                kt, h0, h1 = EXP_UNITS[u]
                if u == 0:
                    pe.wait_ge(m_rows, 32 * (NG * b + g + 1))
                pe.wait_ge(exp_done, past(6 * (NG * b + g) + u - 1))
                view = exp_view(u)
                q0 = min(P * kt, S - 2 * P)
                for h in range(h0, h1):
                    last = nc.tensor.matmul(view[:, h - h0, :], k_stack[:, GH * g + h, P * kt:P * kt + P],
                                            q_stack[:, GH * g + h, q0:S], start=True, stop=True)
                last.then_inc(exp_full, 1)

            def attend(group, b, par, g, kt):
                pe.wait_ge(masked, 4 * group + kt + 1)
                if kt == 0:
                    pe.wait_ge(av_copied, past(group))
                    if g == 0:
                        pe.wait_ge(unit_free, unit_count(b - 1, "F1"))
                p = p_of(kt)
                for j in range(GH):
                    slot, odd = (kt * H + GH * g + j) // 2, j % 2
                    last = nc.tensor.matmul(av_ps[32 * j:32 * j + 32, P * kt:S], v_sb[par][:, slot, odd:odd + 2, :].rearrange("p x d -> p (x d)"),
                                            p[:, j, :], start=kt == 0, stop=kt == TT - 1)
                last.then_inc(av_done, 1)

            def batch(b, par):
                attends, front, prev = flags(b)
                for g in range(NG):
                    for s in range(STEPS):
                        if attends and s in EXP_STEP:
                            exp_scores(b, g, EXP_STEP.index(s))
                        if s < SMAX_STEPS and next_group(b, g):
                            max_scores(b, g, 2 * s)
                            max_scores(b, g, 2 * s + 1)
                        if s == 1 and (g > 0 and attends or g == 0 and prev):
                            attend(NG * b + g - 1, b, par if g else 1 - par, (g - 1) % NG, TT - 1)
                        if attends and s in AV_STEP:
                            attend(NG * b + g, b, par, g, AV_STEP.index(s))
                        for name, ug, us in UNITS:
                            if (g, s) == (ug, us) and (not isinstance(b, int) or has(name, b)):
                                unit(b, name)

            program(pe, batch)

        @block.scalar
        def _(act):
            def split_weight(n, name):
                act.wait_ge(w_in, 16 * 7)
                raw = (p_even if n < 4 else p_odd)[:, :, :].rearrange("p h t -> p (h t)")
                nc.scalar.activation(weights[name][0][:, :, :].rearrange("p c d -> p (c d)"),
                                     raw[:, 512 * (n % 4):512 * (n % 4) + 512], ACT.Copy).then_inc(w_hi, 1)

            for n, name in enumerate(("q", "k", "v", "o", "r", "f", "c")):
                split_weight(n, name)
            act.wait_ge(w_lo, 7)
            act.wait_ge(c_in, 16 * 8)
            act.wait_ge(zeroed, 6)

            def batch(b, par):
                attends, front, prev = flags(b)
                n = b + 1
                for g in range(NG):
                    for s in range(STEPS):
                        here = (g, s)
                        if attends and s in EXP_STEP:
                            u = EXP_STEP.index(s)
                            kt, h0, h1 = EXP_UNITS[u]
                            group = NG * b + g
                            act.wait_ge(exp_full, 6 * group + u + 1)
                            if u in (0, 2):
                                act.wait_ge(av_done, past(4 * group - 1 if u == 0 else 4 * group))
                            if u >= 4:
                                act.wait_ge(av_done, 4 * group + u - 3)
                            view = exp_view(u)
                            valid = S - P * kt
                            view = view[:, :, view.shape[2] - valid:]
                            nc.scalar.activation(p_of(kt)[:, h0:h1, :], view, ACT.Exp, scale=DK ** -0.5).then_inc(exp_done, 1)
                        if s == 2 and (g > 0 and attends or g == 0 and prev):
                            group = NG * b + g - 1
                            act.wait_ge(av_done, 4 * (group + 1))
                            act.wait_ge(gathered, past(GATHER * (2 * b + (g - 1) // 2)))
                            nc.scalar.activation(av_sb[:, (g - 1) % 2, :], av_ps[:, :], ACT.Copy).then_inc(av_copied, 1)
                        if s == 9 and next_group(b, g):
                            act.wait_ge(unit_full, unit_count(b, f"M{g}"))
                            act.wait_ge(m_rows, past(32 * (NG * b + g + 1)))
                            nc.scalar.activation(negm_hi[:, :], unit_ps[0:GH * TT, 0:P], ACT.Copy, scale=-1.0).then_inc(negm_ready, 1)
                        if front:
                            for c in range(DC):
                                if here == (0, 4 + c):
                                    act.wait_ge(unit_full, unit_count(b, f"T{c}"))
                                    if c == 0:
                                        act.wait_ge(mixed, past(2 * n))
                                        act.wait_ge(xn_lo, past(n))
                                    nc.scalar.activation(xnT[:, c, 1:S + 1], unit_ps[:, :], ACT.Copy).then_inc(unit_free, 1)
                            if here == (0, 6):
                                act.wait_ge(unit_free, unit_count(b, "T1"))
                                if ran(b - 1):
                                    act.wait_ge(unit_full, unit_count(b - 1, "F1"))
                                nc.scalar.activation(a_hi[:, :, :], xnT[:, :, 1:S + 1], ACT.Copy).then_inc(xn_hi, 1)
                            for name, at, bias in (("QA", (0, 8), bias_q), ("QB", (0, 10), bias_q), ("KA", (1, 1), bias_k), ("KB", (1, 3), bias_k)):
                                if here == at:
                                    ab = "AB".index(name[1])
                                    act.wait_ge(unit_full, unit_count(b, name))
                                    if ab == 0:
                                        act.wait_ge(qk_lo, past(2 * n + (name[0] == "K")))
                                        act.wait_ge(qk_hi, past(2 * n + (name[0] == "K")))
                                    nc.scalar.activation(rot[:, ab, :], unit_ps[:, :], ACT.Identity, bias=bias[:, ab:ab + 1]).then_inc(unit_free, 1)
                            for k, (at, parts, half1) in enumerate((((0, 13), q_parts, q_loaded), ((1, 10), k_parts, k_loaded))):
                                if here == at:
                                    act.wait_ge(rope_done, 2 * n + k + 1)
                                    for half in range(2):
                                        act.wait_ge(half1[half], past((112, 96)[k] * n))
                                    nc.scalar.activation(parts[:, 0, :, :], rot[:, :, :], ACT.Copy).then_inc(qk_hi, 1)
                            for k, at in enumerate(((0, 14), (1, 11))):
                                if here == at:
                                    act.wait_ge(mixed, 2 * n + k + 1)
                                    if k == 1:
                                        act.wait_ge(unit_full, unit_count(b, "K1"))
                                    elif ran(b - 1):
                                        act.wait_ge(unit_full, unit_count(b - 1, "R1"))
                                    nc.scalar.activation(b_hi[:, :, :], mix[:, :, :], ACT.Copy).then_inc(mix_hi, 1)
                            for c, at in enumerate(((1, 8), (1, 10))):
                                if here == at:
                                    act.wait_ge(unit_full, unit_count(b, f"K{c}"))
                                    act.wait_ge(mixed, 2 * n + 2)
                                    nc.scalar.activation(relu_k[:, c, :], unit_ps[:, :], ACT.Relu).then_inc(unit_free, 1)
                            if here == (2, 6):
                                act.wait_ge(ksq, n + 1)
                                act.wait_ge(unit_full, unit_count(b, "O1" if prev else "K1"))
                                nc.scalar.activation(a_hi[:, :, :], relu_k[:, :, :], ACT.Copy).then_inc(ksq_hi, 1)
                            for k, at in enumerate(((2, 8), (2, 10))):
                                if here == at:
                                    act.wait_ge(unit_full, unit_count(b, f"R{k}"))
                                    act.wait_ge(ksq_lo, n + 1)
                                    act.wait_ge(ksq_hi, n + 1)
                                    nc.scalar.activation(r_sb[:, 2 * k:2 * k + 2, :].rearrange("p a d -> p (a d)"),
                                                         unit_ps[:, :], ACT.Tanh, scale=0.5).then_inc(unit_free, 1)
                        if here == (1, 13) and prev:
                            act.wait_ge(attn_ready, b)
                            act.wait_ge(unit_full, unit_count(b, "V1") if front else unit_count(b - 1, "F1"))
                            nc.scalar.activation(a_hi[:, :, :], tmp[:, :, :], ACT.Copy).then_inc(attn_hi, 1)

            program(act, batch)

        @block.vector
        def _(dve):
            for n, name in enumerate(("q", "k", "v", "o", "r", "f", "c")):
                dve.wait_ge(w_hi, n + 1)
                raw = (p_even if n < 4 else p_odd)[:, :, :].rearrange("p h t -> p (h t)")
                nc.vector.tensor_tensor(weights[name][1][:, :, :].rearrange("p c d -> p (c d)"),
                                        raw[:, 512 * (n % 4):512 * (n % 4) + 512],
                                        weights[name][0][:, :, :].rearrange("p c d -> p (c d)").bitcast(F32),
                                        ALU.subtract).then_inc(w_lo, 1)
            dve.wait_ge(c_in, 16 * 8)
            dve.wait_ge(zeroed, 6)
            dve.wait_ge(consts, 4)

            def batch(b, par):
                attends, front, prev = flags(b)
                n, npar = b + 1, 1 - par
                for g in range(NG):
                    for s in range(STEPS):
                        here = (g, s)
                        if here == (0, 0) and front:
                            dve.wait_ge(x_loaded, 16 * (n + 1))
                            dve.wait_ge(xn_ready, past(n))
                            for a in range(TT):
                                nc.vector.bn_stats(stats[:, a, :], x_in[:, a, :]).then_inc(ln_step, 1)
                            dve.wait_ge(ln_step, (TT + 1) * n + TT)
                            dve.sem_inc(vector_passed, 1)
                            for a in range(TT):
                                last = nc.vector.bn_aggr(mv[:, a, :], stats[:, a, :])
                            last.then_inc(ln_step, 1)
                            dve.wait_ge(ln_step, (TT + 1) * (n + 1))
                            nc.vector.tensor_scalar(veps[:, :], mv[:, :, 1], EPS, None, ALU.add).then_inc(ln_stats, 1)
                        if s < SMAX_STEPS and next_group(b, g):
                            for u in (2 * s, 2 * s + 1):
                                if u == 0:
                                    if g > 0:
                                        dve.wait_ge(unit_full, unit_count(b, f"M{g - 1}"))
                                    elif ran(b - 1):
                                        dve.wait_ge(unit_full, unit_count(b - 1, "M3"))
                                qt = u % TT
                                keys = P * (qt + 1)
                                dve.wait_ge(max_full, 16 * (NG * b + g + 1) + u + 1)
                                dve.sem_inc(vector_passed, 1)
                                nc.vector.tensor_tensor_reduce(out=junk[:, u % 2, 0:keys], in0=max_ps[:, u % 2, 0:keys],
                                                               in1=causal[:, S - keys:S], scale=1.0, scalar=NEG,
                                                               op0=ALU.add, op1=ALU.max,
                                                               accum_out=mx[:, u:u + 1]).then_inc(max_done, 1)
                        if s == 9 and next_group(b, g):
                            dve.wait_ge(negm_ready, NG * b + g + 2)
                            nc.vector.scalar_tensor_tensor(negm_lo[:, :], unit_ps[0:GH * TT, 0:P], -1.0,
                                                           negm_hi[:, :].bitcast(F32), ALU.mult, ALU.subtract).then_inc(unit_free, 1)
                        if front:
                            for k, (at, mu) in enumerate((((0, 13), muk_sb), ((1, 7), mur_sb))):
                                if here == at:
                                    dve.wait_ge(diff_ready, n + 1)
                                    dve.wait_ge(mix_hi, past(2 * n + k))
                                    dve.wait_ge(mix_lo, past(2 * n + k))
                                    for c in range(DC):
                                        last = nc.vector.scalar_tensor_tensor(mix[:, c, :], diff[:, c, :], mu[:, c:c + 1],
                                                                              xnT[:, c, 0:S], ALU.mult, ALU.add)
                                    last.then_inc(mixed, 1)
                            for k, (at, name) in enumerate((((0, 11), "QB"), ((1, 8), "KB"))):
                                if here == at:
                                    dve.wait_ge(unit_free, unit_count(b, name))
                                    dve.wait_ge(rope_done, past(2 * n + k))
                                    if k == 0 and prev:
                                        dve.wait_ge(attn_lo, b - 1)
                                        dve.wait_ge(attn_hi, b - 1)
                                    nc.vector.tensor_tensor(tmp[:, :, :], rot[:, :, :], sin_sb[:, :].unsqueeze(1).to_broadcast([P, 2, S]),
                                                            ALU.mult).then_inc(sin_done, 1)
                                    dve.wait_ge(sin_done, 2 * n + k + 1)
                                    nc.vector.tensor_tensor(rot[:, :, :], rot[:, :, :], cos_sb[:, :].unsqueeze(1).to_broadcast([P, 2, S]),
                                                            ALU.mult).then_inc(rotated, 1)
                            for k, at in enumerate(((1, 5), (1, 6))):
                                if here == at:
                                    dve.wait_ge(unit_full, unit_count(b, f"V{k}"))
                                    dve.wait_ge(av_done, past(16 * (b if prev else 0)))
                                    for a in range(2):
                                        kt = 2 * k + a
                                        last = nc.vector.tensor_tensor(
                                            v_sb[npar][:, kt * H // 2:(kt + 1) * H // 2, 0:3:2, :],
                                            unit_ps[:, D * a:D * a + D].rearrange("p (h x d) -> p h x d", x=2, d=DK),
                                            bv_sb[:, :].rearrange("p (h x d) -> p h x d", x=2, d=DK), ALU.add)
                                    last.then_inc(unit_free, 1)
                            for k, at in enumerate(((3, 3), (3, 5))):
                                if here == at:
                                    dve.wait_ge(unit_full, unit_count(b, f"F{k}"))
                                    dve.wait_ge(r_ready, n + 1)
                                    half = r_sb[:, 2 * k:2 * k + 2, :].rearrange("p a d -> p (a d)")
                                    nc.vector.tensor_tensor(half, half, unit_ps[:, :], ALU.mult).then_inc(unit_free, 1)
                        for at, ok, pair, q in (((0, 8), prev, 2 * b - 1, 1), ((2, 7), attends, 2 * b, 0)):
                            if here == at and ok:
                                dve.wait_ge(gathered, GATHER * (pair + 1))
                                dve.wait_ge(r_written, past(16 * (pair - 1)))
                                nc.vector.reciprocal(rsums[64 * q:64 * q + 64, :], sums[64 * q:64 * q + 64, :]).then_inc(recip_done, 1)
                        if here == (1, 12) and prev:
                            dve.wait_ge(r_read, 32 * 2 * b)
                            if front:
                                dve.wait_ge(rope_done, 2 * n + 2)
                            nc.vector.tensor_tensor(tmp[:, :, :], num[:, :, :], rec[:, :, :], ALU.mult).then_inc(attn_ready, 1)
                        for k, at in enumerate(((2, 3), (2, 5))):
                            if here == at and prev:
                                dve.wait_ge(unit_full, unit_count(b, f"O{k}"))
                                dve.wait_ge(y_ready, b)
                                half = y[npar][:, 2 * k:2 * k + 2, :].rearrange("p a d -> p (a d)")
                                nc.vector.tensor_tensor(half, unit_ps[:, :], half, ALU.add).then_inc(unit_free, 1)

            program(dve, batch)

        @block.gpsimd
        def _(pool):
            nc.gpsimd.memset(ident[:, :], 0.0).then_inc(blank, 1)
            nc.gpsimd.memset(causal[:, :], 0.0).then_inc(blank, 1)
            pool.wait_ge(blank, 2)
            nc.gpsimd.affine_select(out=ident[:, :], in_=ident[:, :], compare_op=ALU.not_equal, fill=1.0,
                                    base=0, pattern=[[-1, P]], channel_multiplier=1).then_inc(consts, 1)
            nc.gpsimd.affine_select(out=causal[:, S - P:S], in_=causal[:, S - P:S], compare_op=ALU.is_ge, fill=NEG,
                                    base=0, pattern=[[-1, P]], channel_multiplier=1).then_inc(consts, 1)
            nc.gpsimd.memset(minus_half[:, :], -0.5).then_inc(consts, 1)
            nc.gpsimd.memset(mx[:, :], 0.0).then_inc(consts, 1)
            nc.gpsimd.memset(xnT[:, :, 0:1], 0.0).then_inc(zeroed, 1)
            for v in v_sb:
                nc.gpsimd.memset(v[:, :, 1, :], 1.0).then_inc(zeroed, 1)
            nc.gpsimd.memset(q_stack[:, :, :].bitcast(F32), 0.0).then_inc(zeroed, 1)
            nc.gpsimd.memset(k_stack[:, :, :].bitcast(F32), 0.0).then_inc(zeroed, 1)
            pool.wait_ge(zeroed, 5)
            nc.gpsimd.memset(k_stack[MROW:MROW + 2, :, :].bitcast(F32), 1.0).then_inc(zeroed, 1)
            pool.wait_ge(c_in, 16 * 8)
            pool.wait_ge(consts, 4)
            pool.wait_ge(zeroed, 6)

            def batch(b, par):
                attends, front, prev = flags(b)
                n, npar = b + 1, 1 - par
                for g in range(NG):
                    for s in range(STEPS):
                        here = (g, s)
                        if here == (0, 0) and front:
                            pool.wait_ge(ln_stats, n + 1)
                            nc.gpsimd.tensor_tensor(rstd[:, :], veps[:, :], minus_half[:, :], ALU.pow).then_inc(ln_rstd, 1)
                            pool.wait_ge(ln_rstd, n + 1)
                            pool.sem_inc(gpsimd_passed, 1)
                            for a in range(TT):
                                last = nc.gpsimd.tensor_scalar(x_in[:, a, :], x_in[:, a, :], mv[:, a, 0:1], rstd[:, a:a + 1],
                                                               ALU.subtract, ALU.mult)
                            last.then_inc(xn_ready, 1)
                        if attends and s in MASK_STEP:
                            kt = MASK_STEP.index(s)
                            pool.wait_ge(exp_done, 6 * (NG * b + g) + LAST_UNIT[kt])
                            pool.sem_inc(gpsimd_passed, 1)
                            diag = p_of(kt)[:, :, 0:P]
                            nc.gpsimd.affine_select(out=diag, in_=diag, compare_op=ALU.is_ge, fill=0.0, base=0,
                                                    pattern=[[0, GH], [1, P]], channel_multiplier=-1).then_inc(masked, 1)
                        if front:
                            if here == (0, 6):
                                pool.wait_ge(xn_hi, n + 1)
                                if ran(b - 1):
                                    pool.wait_ge(unit_full, unit_count(b - 1, "F1"))
                                nc.gpsimd.tensor_tensor(a_lo[:, :, :], xnT[:, :, 1:S + 1], a_hi[:, :, :].bitcast(F32),
                                                        ALU.subtract).then_inc(xn_lo, 1)
                            if here == (0, 7):
                                pool.wait_ge(y_ready, past(n))
                                nc.gpsimd.tensor_tensor(diff[:, :, :], xnT[:, :, 1:S + 1], xnT[:, :, 0:S],
                                                        ALU.subtract).then_inc(diff_ready, 1)
                            for k, at in enumerate(((0, 12), (1, 9))):
                                if here == at:
                                    pool.wait_ge(rotated, 2 * n + k + 1)
                                    nc.gpsimd.tensor_tensor(rot[:, 0, :], rot[:, 0, :], tmp[:, 1, :], ALU.subtract)
                                    nc.gpsimd.tensor_tensor(rot[:, 1, :], rot[:, 1, :], tmp[:, 0, :], ALU.add).then_inc(rope_done, 1)
                            for k, (at, parts, loaded) in enumerate((((0, 13), q_parts, q_loaded), ((1, 10), k_parts, k_loaded))):
                                if here == at:
                                    pool.wait_ge(qk_hi, 2 * n + k + 1)
                                    for half in range(2):
                                        pool.wait_ge(loaded[half], past((112, 96)[k] * n))
                                    nc.gpsimd.tensor_tensor(parts[:, 1, :, :], rot[:, :, :], parts[:, 0, :, :].bitcast(F32),
                                                            ALU.subtract).then_inc(qk_lo, 1)
                            for k, at in enumerate(((0, 14), (1, 12))):
                                if here == at:
                                    pool.wait_ge(mix_hi, 2 * n + k + 1)
                                    if k == 1:
                                        pool.wait_ge(unit_full, unit_count(b, "K1"))
                                    elif ran(b - 1):
                                        pool.wait_ge(unit_full, unit_count(b - 1, "R1"))
                                    nc.gpsimd.tensor_tensor(b_lo[:, :, :], mix[:, :, :], b_hi[:, :, :].bitcast(F32),
                                                            ALU.subtract).then_inc(mix_lo, 1)
                            if here == (2, 0):
                                pool.wait_ge(unit_free, unit_count(b, "K1"))
                                nc.gpsimd.tensor_tensor(relu_k[:, :, :], relu_k[:, :, :], relu_k[:, :, :], ALU.mult).then_inc(ksq, 1)
                            if here == (2, 6):
                                pool.wait_ge(ksq_hi, n + 1)
                                pool.wait_ge(unit_full, unit_count(b, "O1" if prev else "K1"))
                                nc.gpsimd.tensor_tensor(a_lo[:, :, :], relu_k[:, :, :], a_hi[:, :, :].bitcast(F32),
                                                        ALU.subtract).then_inc(ksq_lo, 1)
                            if here == (2, 11):
                                pool.wait_ge(unit_free, unit_count(b, "R1"))
                                pool.sem_inc(gpsimd_passed, 1)
                                nc.gpsimd.tensor_scalar(act_sb[:, :], act_sb[:, :], 0.5, 0.5, ALU.mult, ALU.add).then_inc(r_ready, 1)
                            if here == (3, 4):
                                pool.wait_ge(y_loaded, 16 * (n + 1))
                                nc.gpsimd.tensor_tensor(y[npar][:, :, :], y[npar][:, :, :],
                                                        bo_sb[:, :].unsqueeze(1).to_broadcast([P, TT, D]), ALU.add).then_inc(y_biased, 1)
                            if here == (3, 8):
                                pool.wait_ge(y_biased, n + 1)
                                pool.wait_ge(unit_free, unit_count(b, "F1"))
                                nc.gpsimd.tensor_tensor(y[npar][:, :, :], y[npar][:, :, :], r_sb[:, :, :], ALU.add).then_inc(y_ready, 1)
                        if here == (1, 13) and prev:
                            pool.wait_ge(attn_hi, b)
                            pool.wait_ge(unit_full, unit_count(b, "V1") if front else unit_count(b - 1, "F1"))
                            nc.gpsimd.tensor_tensor(a_lo[:, :, :], tmp[:, :, :], a_hi[:, :, :].bitcast(F32),
                                                    ALU.subtract).then_inc(attn_lo, 1)

            program(pool, batch)


def kernel(**inputs):
    import numpy as _np
    import concourse.bacc as _bacc
    from concourse import mybir as _mybir
    from concourse.bass_utils import run_bass_kernel_spmd as _run

    def get(name):
        return _np.ascontiguousarray(inputs[name])

    half, pair, head = _np.meshgrid(_np.arange(2), _np.arange(8), _np.arange(8), indexing="ij")
    even = ((half * 8 + head) * DK + 2 * pair).ravel()
    perm = _np.concatenate([even, even + 1])
    q, j, d, par = _np.meshgrid(_np.arange(2), _np.arange(4), _np.arange(DK), _np.arange(2), indexing="ij")
    feature = ((GH * (2 * q + par) + j) * DK + d).reshape(P, 2)

    def by_chunk(w):
        return _np.ascontiguousarray(w.T.reshape(DC, P, D).transpose(1, 0, 2))

    inv_freq = (1.0 / _np.float32(10000.0) ** (_np.arange(0, DK, 2, dtype=_np.float32) / _np.float32(DK))).astype(_np.float32)
    angles = _np.arange(S).astype(_np.float32)[None, :] * inv_freq[pair.ravel()][:, None]
    arrays = {
        "x": get("L0_attn_x"),
        "wq": by_chunk(get("L0_attn_Wq")[perm]), "wk": by_chunk(get("L0_attn_Wk")[perm]), "wv": by_chunk(get("L0_attn_Wv")),
        "wo": _np.ascontiguousarray(get("L0_attn_Wo").T[feature]),
        "wr": by_chunk(get("L0_ffn_W_r")), "wf": by_chunk(get("L0_ffn_W_k")), "wc": by_chunk(get("L0_ffn_W_v")),
        "bq": _np.ascontiguousarray(get("L0_attn_bq")[perm].reshape(2, P).T),
        "bk": _np.ascontiguousarray(get("L0_attn_bk")[perm].reshape(2, P).T),
        "bv": get("L0_attn_bv"), "bo": get("L0_attn_bo"),
        "mu_r": _np.ascontiguousarray(get("L0_ffn_mu_r").reshape(DC, P).T),
        "mu_k": _np.ascontiguousarray(get("L0_ffn_mu_k").reshape(DC, P).T),
        "cos_t": _np.cos(angles).astype(_np.float32), "sin_t": _np.sin(angles).astype(_np.float32),
    }
    nc = _bacc.Bacc("TRN2", target_bir_lowering=False, num_devices=1)
    args = {}
    for name, a in arrays.items():
        args[name] = nc.dram_tensor(f"in_{name}", a.shape, _mybir.dt.from_np(a.dtype), kind="ExternalInput").ap()
    out = nc.dram_tensor("out_x", (B, S, D), _mybir.dt.float32, kind="ExternalOutput").ap()
    layer_kernel(nc, **args, out=out)
    r = _run(nc, [{f"in_{name}": a for name, a in arrays.items()}], core_ids=[0])
    return r.results[0]["out_x"]
```

```python
from contextlib import ExitStack

import numpy as np
import concourse.bass as bass
from concourse import mybir

F32 = mybir.dt.float32
F32R = mybir.dt.float32r
BF16 = mybir.dt.bfloat16
ALU = mybir.AluOpType
ACT = mybir.ActivationFunctionType

B, S, D = 32, 512, 256
H, DK = 16, 16
P = 128
TT = S // P
DC = D // P
GH = 4
NG = H // GH
STEPS = 16
MROW = 64
ZROW = 80
GATHER = 16 * 5
KROWS = 96
EPS = 1e-5
NEG = -1e30

UNITS = [("T0", 0, 0), ("T1", 0, 6), ("QA", 0, 8), ("M0", 0, 9), ("QB", 0, 9),
         ("KA", 1, 2), ("KB", 1, 3), ("V0", 1, 5), ("V1", 1, 7), ("K0", 1, 9), ("M1", 1, 10), ("K1", 1, 13),
         ("O0", 2, 2), ("O1", 2, 4), ("R0", 2, 5), ("M2", 2, 8), ("R1", 2, 10),
         ("F0", 3, 3), ("F1", 3, 6), ("M3", 3, 10)]

UNIT_AT = {name: (phase, step) for name, phase, step in UNITS}

AT = {
    "load_x": (0, 14), "layernorm": (3, 8), "rstd": (3, 9), "center": (3, 15), "diff": (0, 1), "rope_q": (0, 11),
    "rope_q_add": (0, 8), "split_q": (0, 12), "rope_k": (1, 9), "rope_k_add": (1, 11), "split_k": (1, 12),
    "mix_k": (0, 15), "mix_k_hi": (1, 1), "mix_k_lo": (0, 12), "mix_r": (1, 3), "mix_r_hi": (1, 13),
    "mix_r_lo": (2, 2), "square": (1, 14), "ksq_split": (2, 3), "sigmoid": (2, 9), "y_bias": (2, 9),
    "y_gate": (3, 14), "gather1": (0, 4), "load1": (0, 0), "load1_keys": (0, 3), "recip1": (0, 9),
    "spread1": (0, 14), "normalize": (1, 11), "attn_split": (1, 11), "load0": (2, 1), "load0_keys": (2, 3),
    "gather0": (2, 2), "store": (2, 4), "recip0": (2, 7), "spread0": (2, 8), "load_y": (2, 15),
}

EXP_STEP = [[1, 1, 2, 4, 4, 4, 5, 7, 9, 10, 11, 12],
            [1, 2, 3, 4, 6, 6, 6, 8, 10, 11, 11, 12],
            [2, 2, 3, 5, 5, 6, 6, 7, 9, 10, 12, 14],
            [1, 1, 2, 4, 5, 5, 5, 8, 10, 10, 12, 13]]
COPY_STEP = [[16],
             [18],
             [18],
             [20]]
AV_STEP = [[7, 10, 12, 16],
           [10, 11, 12, 16],
           [8, 10, 15, 18],
           [8, 10, 15, 16]]
COPY_STEP = [[18]] * 4
MAX_STEP = [[0, 0, 0, 2, 2, 3, 4, 4, 5, 6, 7, 7],
            [0, 0, 0, 1, 2, 3, 3, 4, 5, 7, 7, 8],
            [0, 0, 0, 1, 1, 2, 4, 4, 5, 5, 5, 6],
            [0, 0, 0, 2, 3, 3, 4, 4, 4, 7, 7, 7]]
TURNS = len(MAX_STEP[0])
EXPS = len(EXP_STEP[0])


def due(table, b, g, s, attends, prev):
    found = []
    for late in (1, 0):
        if attends if g >= late else prev:
            found += [(NG * b + g - late, (g - late) % NG, item)
                      for item, at in enumerate(table[(g - late) % NG]) if at == s + STEPS * late]
    return found


def has(unit, b):
    if unit[0] == "M":
        return 0 <= 4 * b + int(unit[1]) + 1 < NG * B
    if unit[0] == "O":
        return b >= 1
    return b + 1 < B


def unit_count(b, unit):
    names = [u for u, _, _ in UNITS]
    if isinstance(b, int):
        before = sum(has(u, a) for a in range(-1, b) for u in names)
        return before + sum(has(u, b) for u in names[:names.index(unit) + 1])
    first = sum(has(u, a) for a in (-1, 0) for u in names)
    return b * len(names) + (first - len(names) + names.index(unit) + 1)


def ran(b):
    return not isinstance(b, int) or b >= -1


def past(count):
    return max(count, 0) if isinstance(count, int) else count


def layer_kernel(nc, x, wq, wk, wv, wo, wr, wf, wc, bq, bk, bv, bo, mu_r, mu_k, cos_t, sin_t, out):
    with ExitStack() as ctx:
        def sb(name, shape, dt=F32):
            return ctx.enter_context(nc.sbuf_tensor(name, shape, dt))

        def psum(name, shape):
            return ctx.enter_context(nc.psum_tensor(name, shape, F32))

        def sem(name):
            return ctx.enter_context(nc.semaphore(name))

        max_ps = psum("max_ps", [P, 3, S])
        exp_ps = psum("exp_ps", [P, 3, S])
        av_ps = psum("av_ps", [P, S])
        unit_ps = psum("unit_ps", [P, S])

        weights = {}
        for name in ("q", "k", "v", "o", "r", "f", "c"):
            weights[name] = [sb(f"w{name}_{part}", [P, DC, D], F32R) for part in ("hi", "lo")]
        cos_sb, sin_sb = sb("cos_sb", [P, S]), sb("sin_sb", [P, S])
        ident, ident_bf = sb("ident", [P, P]), sb("ident_bf", [P, P], BF16)
        causal = sb("causal", [P, S], BF16)
        bias_q, bias_k = sb("bias_q", [P, 2]), sb("bias_k", [P, 2])
        mur_sb, muk_sb = sb("mur_sb", [P, DC]), sb("muk_sb", [P, DC])
        bv_sb, bo_sb = sb("bv_sb", [P, D]), sb("bo_sb", [P, D])
        minus_half = sb("minus_half", [P, TT])

        q_stack, k_stack = sb("q_stack", [KROWS, H, S], F32R), sb("k_stack", [KROWS, H, S], F32R)
        p_even = sb("p_even", [P, GH, S])
        p_odd = sb("p_odd", [P, GH, S - P])
        v_sb = [sb(f"v{i}", [P, TT * H, 2, DK]) for i in range(2)]
        mx = sb("mx", [P, 2 * GH * TT])
        negm_hi, negm_lo = sb("negm_hi", [GH * TT, P], F32R), sb("negm_lo", [GH * TT, P], F32R)
        av_sb = sb("av_sb", [P, 2, S])
        num = sb("num", [P, 2, S])
        sums = sb("sums", [P, 64])
        rec = sb("rec", [P, 2, S])
        rscratch = nc.dram_tensor("rscratch", (2, GH, 2, S), F32, kind="Internal").ap()

        x_in = sb("x_in", [P, TT, D])
        stats, mv = sb("stats", [P, TT, 6]), sb("mv", [P, TT, 2])
        veps, rstd = sb("veps", [P, TT]), sb("rstd", [P, TT])
        xnT = sb("xnT", [P, DC, S + 1])
        a_hi, a_lo = sb("a_hi", [P, DC, S], F32R), sb("a_lo", [P, DC, S], F32R)
        b_hi, b_lo = sb("b_hi", [P, DC, S], F32R), sb("b_lo", [P, DC, S], F32R)
        mix = sb("mix", [P, DC, S])
        act_sb = sb("act_sb", [P, DC * S])
        diff = act_sb[:, :].rearrange("p (c t) -> p c t", c=DC)
        relu_k = diff
        r_sb = act_sb[:, :].rearrange("p (a d) -> p a d", a=TT)
        rot = sb("rot", [P, 2, S])
        tmp = sb("tmp", [P, 2, S])
        q_parts, k_parts = sb("q_parts", [P, 2, 2, S], F32R), sb("k_parts", [P, 2, 2, S], F32R)
        y = [sb(f"y{i}", [P, TT, D]) for i in range(2)]

        w_in, c_in = sem("w_in"), sem("c_in")
        w_hi, w_lo, consts, zeroed, ones, blank = (sem(n) for n in ("w_hi", "w_lo", "consts", "zeroed", "ones", "blank"))
        unit_full, unit_free = sem("unit_full"), sem("unit_free")
        max_full, max_done = sem("max_full"), sem("max_done")
        exp_full, exp_done = sem("exp_full"), sem("exp_done")
        av_done, av_copied = sem("av_done"), sem("av_copied")
        negm_ready, m_rows = sem("negm_ready"), sem("m_rows")
        q_loaded = [sem(f"q_loaded{i}") for i in range(2)]
        k_loaded = [sem(f"k_loaded{i}") for i in range(2)]
        gathered, recip_done, r_written, r_read = sem("gathered"), sem("recip_done"), sem("r_written"), sem("r_read")
        attn_ready, attn_hi, attn_lo = sem("attn_ready"), sem("attn_hi"), sem("attn_lo")
        stored = sem("stored")
        x_loaded, y_loaded, y_biased, y_ready = sem("x_loaded"), sem("y_loaded"), sem("y_biased"), sem("y_ready")
        ln_step, ln_stats, ln_rstd, xn_ready = sem("ln_step"), sem("ln_stats"), sem("ln_rstd"), sem("xn_ready")
        xn_hi, diff_ready = sem("xn_hi"), sem("diff_ready")
        mixed, mix_hi, mix_lo = sem("mixed"), sem("mix_hi"), sem("mix_lo")
        sin_done, rotated, rope_done, qk_hi, qk_lo = (sem(n) for n in ("sin_done", "rotated", "rope_done", "qk_hi", "qk_lo"))
        ksq, ksq_hi, ksq_lo, r_ready = sem("ksq"), sem("ksq_hi"), sem("ksq_lo"), sem("r_ready")

        sync_passed, vector_passed, gpsimd_passed = sem("sync_passed"), sem("vector_passed"), sem("gpsimd_passed")

        def p_of(kt):
            t = p_odd if kt % 2 else p_even
            return t[:, :, 0:S - P * kt]

        def program(eng, batch):
            batch(-1, 1)
            batch(0, 0)
            with eng.Fori(0, (B - 4) // 2) as i:
                batch(2 * i + 1, 1)
                batch(2 * i + 2, 0)
            for b in range(B - 3, B + 1):
                batch(b, b % 2)

        def flags(b):
            if isinstance(b, int):
                return 0 <= b < B, b + 1 < B, b >= 1, b + 2 < B
            return True, True, True, True

        def next_group(b, g):
            return not isinstance(b, int) or 0 <= NG * b + g + 1 < NG * B

        EXP_UNITS = [(kt, h, h + 1) for kt in (0, 1) for h in range(GH)] + [(kt, h, h + 2) for kt in (2, 3) for h in (0, 2)]
        LAST_UNIT = [4, 8, 10, 12]
        TURN_TILES = [(0, 1), (2,), (3,)]

        def exp_view(u):
            kt, bank = EXP_UNITS[u][0], exp_ps[:, u % 3, :]
            if kt < 2:
                return bank[:, 0:S - P * kt].unsqueeze(1)
            return bank.rearrange("p (h t) -> p h t", h=2)

        block = ctx.enter_context(nc.Block())

        @block.sync
        def _(sp):
            x_tiles = x.rearrange("b (a p) d -> b p a d", p=P)
            out_tiles = out.rearrange("b (a p) d -> b p a d", p=P)

            def row(ap, b):
                return ap[b] if isinstance(b, int) else ap[bass.ds(b, 1)].rearrange("o p a d -> p (o a) d")

            sp.dma_start(x_in[:, :, :], row(x_tiles, 0)).then_inc(x_loaded, 16)
            for n, (name, w) in enumerate((("q", wq), ("k", wk), ("v", wv), ("o", wo), ("r", wr), ("f", wf), ("c", wc))):
                raw = (p_even if n < 4 else p_odd)[:, :, :].rearrange("p h t -> p (h t)")
                sp.dma_start(raw[:, 512 * (n % 4):512 * (n % 4) + 512], w.rearrange("p c d -> p (c d)")).then_inc(w_in, 16)
            for dst, src in ((cos_sb, cos_t), (sin_sb, sin_t), (bias_q, bq), (bias_k, bk), (mur_sb, mu_r), (muk_sb, mu_k)):
                sp.dma_start(dst[:, :], src).then_inc(c_in, 16)
            for dst, src in ((bv_sb, bv), (bo_sb, bo)):
                sp.dma_start(dst[:, :], src.unsqueeze(0).to_broadcast([P, D])).then_inc(c_in, 16)

            def stack_rows(stack, row, rows, head, heads):
                return stack[row:row + rows, head:head + heads, :].rearrange("r h t -> r (h t)").bitcast(F32)

            def load_stack(stack, parts, order, half, loaded):
                for term, part in enumerate(order):
                    for ab in range(2):
                        row = 16 * term + 8 * ab
                        sp.dma_start(stack_rows(stack, row, 8, 8 * half, 8),
                                     parts[64 * half:64 * half + 64, part, ab, :].bitcast(F32)).then_inc(loaded, 16)

            def load_queries(n, half):
                sp.wait_ge(qk_hi, 2 * n + 1)
                sp.sem_inc(sync_passed, 1)
                sp.wait_ge(qk_lo, 2 * n + 1)
                sp.sem_inc(sync_passed, 1)
                load_stack(q_stack, q_parts, (0, 1, 0), half, q_loaded[half])
                sp.dma_start(stack_rows(q_stack, MROW, 2, 8 * half, 8), stack_rows(q_stack, ZROW, 2, 8 * half, 8)).then_inc(q_loaded[half], 16)

            def load_keys(n, half):
                sp.wait_ge(qk_hi, 2 * n + 2)
                sp.sem_inc(sync_passed, 1)
                sp.wait_ge(qk_lo, 2 * n + 2)
                sp.sem_inc(sync_passed, 1)
                load_stack(k_stack, k_parts, (0, 0, 1), half, k_loaded[half])

            def gather(b, q):
                pair = 2 * b + q
                sp.wait_ge(av_copied, 2 * (pair + 1))
                sp.sem_inc(sync_passed, 1)
                sp.wait_ge(attn_ready, past(b))
                sp.sem_inc(sync_passed, 1)
                sp.wait_ge(r_written, past(16 * (pair - 1)))
                sp.sem_inc(sync_passed, 1)
                for j in range(GH):
                    sp.dma_start(num[64 * q + 16 * j:64 * q + 16 * j + 16, :, :],
                                 av_sb[32 * j:32 * j + 16, :, :]).then_inc(gathered, 16)
                sp.dma_start(sums[64 * q:64 * q + 64, :], av_sb[16:P:32, :, :]).then_inc(gathered, 16)

            def spread(b, q):
                pair = 2 * b + q
                sp.wait_ge(recip_done, pair + 1)
                sp.sem_inc(sync_passed, 1)
                sp.wait_ge(r_read, past(16 * (pair - 1)))
                sp.sem_inc(sync_passed, 1)
                sp.wait_ge(attn_ready, past(b))
                sp.dma_start(rscratch[q].rearrange("h g (a t) -> (h g a) t", a=8), sums[64 * q:64 * q + 64, :]).then_inc(r_written, 16)
                sp.wait_ge(r_written, 16 * (pair + 1))
                sp.sem_inc(sync_passed, 1)
                sp.dma_start(rec[64 * q:64 * q + 64, :, :],
                             rscratch[q].unsqueeze(1).to_broadcast([GH, DK, 2, S])).then_inc(r_read, 16)

            def batch(b, par):
                attends, front, prev, ahead = flags(b)
                n, ypar = b + 1, 1 - par
                for g in range(NG):
                    for s in range(STEPS):
                        if (g, s) == AT["load_x"] and ahead:
                            sp.wait_ge(unit_full, unit_count(b, "T1"))
                            sp.dma_start(x_in[:, :, :], row(x_tiles, b + 2)).then_inc(x_loaded, 16)
                        if (g, s) == AT["gather1"] and prev:
                            gather(b - 1, 1)
                        if (g, s) == AT["load1"] and attends:
                            sp.wait_ge(exp_full, past(NG * EXPS * b))
                            sp.sem_inc(sync_passed, 1)
                            load_queries(b, 1)
                        if (g, s) == AT["load1_keys"] and attends:
                            sp.wait_ge(exp_full, past(NG * EXPS * b))
                            sp.sem_inc(sync_passed, 1)
                            load_keys(b, 1)
                        if (g, s) == AT["gather0"] and attends:
                            gather(b, 0)
                        if (g, s) == AT["load0"] and front:
                            sp.wait_ge(exp_full, past(EXPS * (NG * b + 2)))
                            sp.sem_inc(sync_passed, 1)
                            load_queries(n, 0)
                        if (g, s) == AT["load0_keys"] and front:
                            sp.wait_ge(exp_full, past(EXPS * (NG * b + 2)))
                            sp.sem_inc(sync_passed, 1)
                            load_keys(n, 0)
                        if (g, s) == AT["store"] and prev:
                            sp.wait_ge(unit_free, unit_count(b, "O1"))
                            sp.dma_start(row(out_tiles, b - 1), y[ypar][:, :, :]).then_inc(stored, 16)
                        if (g, s) == AT["load_y"] and front:
                            sp.wait_ge(stored, past(16 * (b if prev else 0)))
                            sp.dma_start(y[ypar][:, :, :], row(x_tiles, n)).then_inc(y_loaded, 16)
                        if (g, s) == UNIT_AT[f"M{g}"] and next_group(b, g):
                            nxt = NG * b + g + 1
                            h0 = (GH * (g + 1)) % H
                            sp.wait_ge(negm_ready, nxt + 1)
                            sp.dma_start(stack_rows(q_stack, MROW, 1, h0, GH), negm_hi[:, :].bitcast(F32)).then_inc(m_rows, 16)
                            sp.wait_ge(unit_free, unit_count(b, f"M{g}"))
                            sp.dma_start(stack_rows(q_stack, MROW + 1, 1, h0, GH), negm_lo[:, :].bitcast(F32)).then_inc(m_rows, 16)
                        if (g, s) == AT["spread1"] and prev:
                            spread(b - 1, 1)
                        if (g, s) == AT["spread0"] and attends:
                            spread(b, 0)

            sp.wait_ge(consts, 8)
            sp.wait_ge(zeroed, 2)
            sp.dma_start(stack_rows(k_stack, MROW, 2, 0, H), v_sb[0][:, 0:2 * H * S // P // DK, 1, :]).then_inc(ones, 16)
            sp.wait_ge(ones, 16)
            program(sp, batch)
            sp.wait_ge(stored, 16 * B)

        @block.tensor
        def _(pe):
            pe.wait_ge(consts, 8)
            pe.wait_ge(w_hi, 7)
            pe.wait_ge(w_lo, 7)

            def claim(b, unit):
                pe.wait_ge(unit_free, past(unit_count(b, unit) - 1))

            def project(hi_lo, w, token_tiles=None, cols=None):
                terms = [(c, i, j) for c in range(DC) for i, j in ((0, 0), (0, 1), (1, 0))]
                if token_tiles is None:
                    for m, (c, i, j) in enumerate(terms):
                        last = nc.tensor.matmul(unit_ps[:, :], weights[w][j][:, c, cols:cols + P], hi_lo[i][:, c, :],
                                                start=m == 0, stop=m == 5)
                else:
                    for k, a in enumerate(token_tiles):
                        for m, (c, i, j) in enumerate(terms):
                            last = nc.tensor.matmul(unit_ps[:, D * k:D * k + D], hi_lo[i][:, c, P * a:P * a + P],
                                                    weights[w][j][:, c, :], start=m == 0, stop=m == 5)
                last.then_inc(unit_full, 1)

            def unit(b, name):
                claim(b, name)
                n, kind, k = b + 1, name[0], name[1:]
                if kind == "T":
                    pe.wait_ge(xn_ready, n + 1)
                    for a in range(TT):
                        last = nc.tensor.transpose(unit_ps[:, P * a:P * a + P], x_in[:, a, P * int(k):P * int(k) + P], ident[:, :])
                    last.then_inc(unit_full, 1)
                elif name in ("QA", "QB", "KA", "KB"):
                    project((a_hi, a_lo), kind.lower(), cols=P * "AB".index(k))
                elif kind == "V":
                    project((a_hi, a_lo), "v", token_tiles=(2 * int(k), 2 * int(k) + 1))
                elif kind == "K":
                    pe.wait_ge(mix_hi, 2 * n + 1)
                    pe.wait_ge(mix_lo, 2 * n + 1)
                    project((b_hi, b_lo), "f", cols=P * int(k))
                elif kind == "R":
                    pe.wait_ge(mix_hi, 2 * n + 2)
                    pe.wait_ge(mix_lo, 2 * n + 2)
                    project((b_hi, b_lo), "r", token_tiles=(2 * int(k), 2 * int(k) + 1))
                elif kind == "F":
                    pe.wait_ge(ksq_hi, n + 1)
                    pe.wait_ge(ksq_lo, n + 1)
                    project((a_hi, a_lo), "c", token_tiles=(2 * int(k), 2 * int(k) + 1))
                elif kind == "O":
                    pe.wait_ge(attn_hi, b)
                    pe.wait_ge(attn_lo, b)
                    project((a_hi, a_lo), "o", token_tiles=(2 * int(k), 2 * int(k) + 1))
                elif kind == "M":
                    pe.wait_ge(max_done, TURNS * (NG * b + int(k) + 2))
                    nc.tensor.transpose(unit_ps[0:2 * GH * TT, 0:P], mx[:, :], ident[:, :]).then_inc(unit_full, 1)

            def max_scores(b, g, turn):
                nxt = TURNS * (NG * b + g + 1) + turn
                h, tiles = (GH * (g + 1)) % H + turn // 3, TURN_TILES[turn % 3]
                if turn == 0:
                    half = h // 8
                    nb = b + 1 if g == NG - 1 else b
                    pe.wait_ge(q_loaded[half], 112 * (nb + 1))
                    pe.wait_ge(k_loaded[half], 96 * (nb + 1))
                pe.wait_ge(max_done, past(nxt - 2))
                for i, qt in enumerate(tiles):
                    keys = max(2 * P, P * (qt + 1))
                    last = nc.tensor.matmul(max_ps[:, turn % 3, 2 * P * i:2 * P * i + keys], q_stack[:, h, P * qt:P * qt + P],
                                            k_stack[:, h, 0:keys], start=True, stop=True)
                last.then_inc(max_full, 1)

            def exp_scores(group, g, u):
                kt, h0, h1 = EXP_UNITS[u]
                if u == 0:
                    pe.wait_ge(m_rows, 32 * (group + 1))
                pe.wait_ge(exp_done, past(EXPS * group + u - 2))
                view = exp_view(u)
                q0 = min(P * kt, S - 2 * P)
                for h in range(h0, h1):
                    nc.tensor.matmul(view[:, h - h0, :], k_stack[:, GH * g + h, P * kt:P * kt + P],
                                     q_stack[:, GH * g + h, q0:S], start=True, stop=False)
                    last = nc.tensor.matmul(view[:, h - h0, P * kt - q0:P * kt - q0 + P], causal[:, S - P:S], ident_bf[:, :],
                                            start=False, stop=True)
                last.then_inc(exp_full, 1)

            def attend(group, b, par, g, kt):
                pe.wait_ge(exp_done, EXPS * group + LAST_UNIT[kt])
                if kt == 0:
                    pe.wait_ge(av_copied, past(group))
                    if g == 0:
                        pe.wait_ge(unit_free, unit_count(b - 1, "F1"))
                p = p_of(kt)
                for j in range(GH):
                    last = nc.tensor.matmul(av_ps[32 * j:32 * j + 32, P * kt:S],
                                            v_sb[par][:, kt * H + GH * g + j, :, :].rearrange("p x d -> p (x d)"),
                                            p[:, j, :], start=kt == 0, stop=kt == TT - 1)
                last.then_inc(av_done, 1)

            def batch(b, par):
                attends, front, prev, ahead = flags(b)
                for g in range(NG):
                    for s in range(STEPS):
                        for group, g2, u in due(EXP_STEP, b, g, s, attends, prev):
                            exp_scores(group, g2, u)
                        if next_group(b, g):
                            for turn, at in enumerate(MAX_STEP[g]):
                                if at == s:
                                    max_scores(b, g, turn)
                        for group, g2, kt in due(AV_STEP, b, g, s, attends, prev):
                            attend(group, b, par if g2 <= g else 1 - par, g2, kt)
                        for name, ug, us in UNITS:
                            if (g, s) == (ug, us) and (not isinstance(b, int) or has(name, b)):
                                unit(b, name)

            program(pe, batch)

        @block.scalar
        def _(act):
            def split_weight(n, name):
                act.wait_ge(w_in, 16 * 7)
                raw = (p_even if n < 4 else p_odd)[:, :, :].rearrange("p h t -> p (h t)")
                nc.scalar.activation(weights[name][0][:, :, :].rearrange("p c d -> p (c d)"),
                                     raw[:, 512 * (n % 4):512 * (n % 4) + 512], ACT.Copy).then_inc(w_hi, 1)

            for n, name in enumerate(("q", "k", "v", "o", "r", "f", "c")):
                split_weight(n, name)
            act.wait_ge(w_lo, 7)
            act.wait_ge(c_in, 16 * 8)
            act.wait_ge(consts, 8)

            def batch(b, par):
                attends, front, prev, ahead = flags(b)
                n = b + 1
                for g in range(NG):
                    for s in range(STEPS):
                        here = (g, s)
                        for group, g2, u in due(EXP_STEP, b, g, s, attends, prev):
                            kt, h0, h1 = EXP_UNITS[u]
                            act.wait_ge(exp_full, EXPS * group + u + 1)
                            if u in (0, 4):
                                act.wait_ge(av_done, past(4 * group - 1 if u == 0 else 4 * group))
                            if u in (8, 10):
                                act.wait_ge(av_done, 4 * group + kt - 1)
                            view = exp_view(u)
                            valid = S - P * kt
                            view = view[:, :, view.shape[2] - valid:]
                            nc.scalar.activation(p_of(kt)[:, h0:h1, :], view, ACT.Exp, scale=DK ** -0.5).then_inc(exp_done, 1)
                        for group, g2, _ in due(COPY_STEP, b, g, s, attends, prev):
                            act.wait_ge(av_done, 4 * (group + 1))
                            act.wait_ge(gathered, past(GATHER * (2 * b + (g2 if g2 <= g else g2 - NG) // 2)))
                            nc.scalar.activation(av_sb[:, g2 % 2, :], av_ps[:, :], ACT.Copy).then_inc(av_copied, 1)
                        if (g, s) == UNIT_AT[f"M{g}"] and next_group(b, g):
                            act.wait_ge(unit_full, unit_count(b, f"M{g}"))
                            act.wait_ge(m_rows, past(32 * (NG * b + g + 1)))
                            nc.scalar.activation(negm_hi[:, :], unit_ps[0:GH * TT, 0:P], ACT.Copy, scale=-1.0).then_inc(negm_ready, 1)
                        if front:
                            for c in range(DC):
                                if here == UNIT_AT[f"T{c}"]:
                                    act.wait_ge(unit_full, unit_count(b, f"T{c}"))
                                    if c == 0:
                                        act.wait_ge(mixed, past(2 * n))
                                        if ran(b - 1):
                                            act.wait_ge(unit_full, unit_count(b - 1, "F1"))
                                    nc.scalar.activation(a_hi[:, c, :], unit_ps[:, :], ACT.Copy)
                                    nc.scalar.activation(xnT[:, c, 1:S + 1], unit_ps[:, :], ACT.Copy).then_inc(xn_hi, 1)
                            for name, bias in (("QA", bias_q), ("QB", bias_q), ("KA", bias_k), ("KB", bias_k)):
                                if here == UNIT_AT[name]:
                                    ab = "AB".index(name[1])
                                    act.wait_ge(unit_full, unit_count(b, name))
                                    if ab == 0:
                                        act.wait_ge(qk_lo, past(2 * n + (name[0] == "K")))
                                        act.wait_ge(qk_hi, past(2 * n + (name[0] == "K")))
                                    nc.scalar.activation(rot[:, ab, :], unit_ps[:, :], ACT.Identity, bias=bias[:, ab:ab + 1]).then_inc(unit_free, 1)
                            for k, (at, parts, half1) in enumerate(((AT["split_q"], q_parts, q_loaded), (AT["split_k"], k_parts, k_loaded))):
                                if here == at:
                                    act.wait_ge(rope_done, 2 * n + k + 1)
                                    for half in range(2):
                                        act.wait_ge(half1[half], past((112, 96)[k] * n))
                                    nc.scalar.activation(parts[:, 0, :, :], rot[:, :, :], ACT.Copy).then_inc(qk_hi, 1)
                            for k, at in enumerate((AT["mix_k_hi"], AT["mix_r_hi"])):
                                if here == at:
                                    act.wait_ge(mixed, 2 * n + k + 1)
                                    if k == 1:
                                        act.wait_ge(unit_full, unit_count(b, "K1"))
                                    elif ran(b - 1):
                                        act.wait_ge(unit_full, unit_count(b - 1, "R1"))
                                    nc.scalar.activation(b_hi[:, :, :], mix[:, :, :], ACT.Copy).then_inc(mix_hi, 1)
                            for c, at in enumerate((UNIT_AT["K0"], UNIT_AT["K1"])):
                                if here == at:
                                    act.wait_ge(unit_full, unit_count(b, f"K{c}"))
                                    act.wait_ge(mixed, 2 * n + 2)
                                    nc.scalar.activation(relu_k[:, c, :], unit_ps[:, :], ACT.Relu).then_inc(unit_free, 1)
                            if here == AT["square"]:
                                act.wait_ge(unit_free, unit_count(b, "K1"))
                                nc.scalar.activation(relu_k[:, :, :], relu_k[:, :, :], ACT.Square).then_inc(ksq, 1)
                            if here == AT["ksq_split"]:
                                act.wait_ge(ksq, n + 1)
                                act.wait_ge(unit_full, unit_count(b, "O1" if prev else "K1"))
                                nc.scalar.activation(a_hi[:, :, :], relu_k[:, :, :], ACT.Copy).then_inc(ksq_hi, 1)
                            for k, at in enumerate((UNIT_AT["R0"], UNIT_AT["R1"])):
                                if here == at:
                                    act.wait_ge(unit_full, unit_count(b, f"R{k}"))
                                    act.wait_ge(ksq_lo, n + 1)
                                    act.wait_ge(ksq_hi, n + 1)
                                    nc.scalar.activation(r_sb[:, 2 * k:2 * k + 2, :].rearrange("p a d -> p (a d)"),
                                                         unit_ps[:, :], ACT.Tanh, scale=0.5).then_inc(unit_free, 1)
                        if here == AT["attn_split"] and prev:
                            act.wait_ge(attn_ready, b)
                            act.wait_ge(unit_full, unit_count(b, "V1") if front else unit_count(b - 1, "F1"))
                            nc.scalar.activation(a_hi[:, :, :], tmp[:, :, :], ACT.Copy).then_inc(attn_hi, 1)

            program(act, batch)

        @block.vector
        def _(dve):
            def statistics(m):
                dve.wait_ge(x_loaded, 16 * (m + 1))
                dve.wait_ge(xn_ready, m)
                for a in range(TT):
                    nc.vector.bn_stats(stats[:, a, :], x_in[:, a, :]).then_inc(ln_step, 1)
                dve.wait_ge(ln_step, (TT + 1) * m + TT)
                dve.sem_inc(vector_passed, 1)
                for a in range(TT):
                    last = nc.vector.bn_aggr(mv[:, a, :], stats[:, a, :])
                last.then_inc(ln_step, 1)
                dve.wait_ge(ln_step, (TT + 1) * (m + 1))
                nc.vector.tensor_scalar(veps[:, :], mv[:, :, 1], EPS, None, ALU.add).then_inc(ln_stats, 1)

            def center(m):
                dve.wait_ge(ln_rstd, m + 1)
                for a in range(TT):
                    last = nc.vector.tensor_scalar(x_in[:, a, :], x_in[:, a, :], mv[:, a, 0:1], rstd[:, a:a + 1],
                                                   ALU.subtract, ALU.mult)
                last.then_inc(xn_ready, 1)

            def batch(b, par):
                attends, front, prev, ahead = flags(b)
                n, npar = b + 1, 1 - par
                for g in range(NG):
                    for s in range(STEPS):
                        here = (g, s)
                        if here == AT["layernorm"] and ahead:
                            statistics(b + 2)
                        if here == AT["center"] and ahead:
                            center(b + 2)
                        for turn, at in enumerate(MAX_STEP[g]):
                            if at == s and next_group(b, g):
                                if turn == 0:
                                    if g > 0:
                                        dve.wait_ge(unit_full, unit_count(b, f"M{g - 1}"))
                                    elif ran(b - 1):
                                        dve.wait_ge(unit_full, unit_count(b - 1, "M3"))
                                dve.wait_ge(max_full, TURNS * (NG * b + g + 1) + turn + 1)
                                dve.sem_inc(vector_passed, 1)
                                for i, qt in enumerate(TURN_TILES[turn % 3]):
                                    keys, col, u = P * (qt + 1), 2 * P * i, TT * (turn // 3) + qt
                                    last = nc.vector.tensor_tensor_reduce(out=max_ps[:, turn % 3, col:col + keys],
                                                                          in0=max_ps[:, turn % 3, col:col + keys],
                                                                          in1=causal[:, S - keys:S], scale=1.0, scalar=NEG,
                                                                          op0=ALU.add, op1=ALU.max, accum_out=mx[:, u:u + 1])
                                last.then_inc(max_done, 1)
                        if (g, s) == UNIT_AT[f"M{g}"] and next_group(b, g):
                            dve.wait_ge(negm_ready, NG * b + g + 2)
                            nc.vector.scalar_tensor_tensor(negm_lo[:, :], unit_ps[0:GH * TT, 0:P], -1.0,
                                                           negm_hi[:, :].bitcast(F32), ALU.mult, ALU.subtract).then_inc(unit_free, 1)
                        if front:
                            for k, (at, mu) in enumerate(((AT["mix_k"], muk_sb), (AT["mix_r"], mur_sb))):
                                if here == at:
                                    dve.wait_ge(diff_ready, n + 1)
                                    dve.wait_ge(mix_hi, past(2 * n + k))
                                    dve.wait_ge(mix_lo, past(2 * n + k))
                                    for c in range(DC):
                                        last = nc.vector.scalar_tensor_tensor(mix[:, c, :], diff[:, c, :], mu[:, c:c + 1],
                                                                              xnT[:, c, 0:S], ALU.mult, ALU.add)
                                    last.then_inc(mixed, 1)
                            for k, (at, name) in enumerate(((AT["rope_q"], "QB"), (AT["rope_k"], "KB"))):
                                if here == at:
                                    dve.wait_ge(unit_free, unit_count(b, name))
                                    dve.wait_ge(rope_done, past(2 * n + k))
                                    if k == 0 and prev:
                                        dve.wait_ge(attn_lo, b - 1)
                                        dve.wait_ge(attn_hi, b - 1)
                                    nc.vector.tensor_tensor(tmp[:, :, :], rot[:, :, :], sin_sb[:, :].unsqueeze(1).to_broadcast([P, 2, S]),
                                                            ALU.mult).then_inc(sin_done, 1)
                                    dve.wait_ge(sin_done, 2 * n + k + 1)
                                    nc.vector.tensor_tensor(rot[:, :, :], rot[:, :, :], cos_sb[:, :].unsqueeze(1).to_broadcast([P, 2, S]),
                                                            ALU.mult).then_inc(rotated, 1)
                            for c in range(DC):
                                if here == UNIT_AT[f"T{c}"]:
                                    dve.wait_ge(xn_hi, DC * n + c + 1)
                                    if ran(b - 1):
                                        dve.wait_ge(unit_full, unit_count(b - 1, "F1"))
                                    nc.vector.tensor_tensor(a_lo[:, c, :], unit_ps[:, :], a_hi[:, c, :].bitcast(F32),
                                                            ALU.subtract).then_inc(unit_free, 1)
                            for k, at in enumerate((UNIT_AT["V0"], UNIT_AT["V1"])):
                                if here == at:
                                    dve.wait_ge(unit_full, unit_count(b, f"V{k}"))
                                    dve.wait_ge(av_done, past(16 * (b if prev else 0)))
                                    for a in range(2):
                                        kt = 2 * k + a
                                        last = nc.vector.tensor_tensor(
                                            v_sb[npar][:, kt * H:(kt + 1) * H, 0, :],
                                            unit_ps[:, D * a:D * a + D].rearrange("p (h d) -> p h d", d=DK),
                                            bv_sb[:, :].rearrange("p (h d) -> p h d", d=DK), ALU.add)
                                    last.then_inc(unit_free, 1)
                            for k, at in enumerate((UNIT_AT["F0"], UNIT_AT["F1"])):
                                if here == at:
                                    dve.wait_ge(unit_full, unit_count(b, f"F{k}"))
                                    dve.wait_ge(r_ready, n + 1)
                                    half = r_sb[:, 2 * k:2 * k + 2, :].rearrange("p a d -> p (a d)")
                                    nc.vector.tensor_tensor(half, half, unit_ps[:, :], ALU.mult).then_inc(unit_free, 1)
                        for at, ok, pair, q in ((AT["recip1"], prev, 2 * b - 1, 1), (AT["recip0"], attends, 2 * b, 0)):
                            if here == at and ok:
                                dve.wait_ge(gathered, GATHER * (pair + 1))
                                nc.vector.reciprocal(sums[64 * q:64 * q + 64, :], sums[64 * q:64 * q + 64, :]).then_inc(recip_done, 1)
                        if here == AT["normalize"] and prev:
                            dve.wait_ge(r_read, 16 * 2 * b)
                            if front:
                                dve.wait_ge(rope_done, 2 * n + 2)
                            nc.vector.tensor_tensor(tmp[:, :, :], num[:, :, :], rec[:, :, :], ALU.mult).then_inc(attn_ready, 1)
                        for k, at in enumerate((UNIT_AT["O0"], UNIT_AT["O1"])):
                            if here == at and prev:
                                dve.wait_ge(unit_full, unit_count(b, f"O{k}"))
                                dve.wait_ge(y_ready, b)
                                half = y[npar][:, 2 * k:2 * k + 2, :].rearrange("p a d -> p (a d)")
                                nc.vector.tensor_tensor(half, unit_ps[:, :], half, ALU.add).then_inc(unit_free, 1)

            statistics(0)
            for n, name in enumerate(("q", "k", "v", "o", "r", "f", "c")):
                dve.wait_ge(w_hi, n + 1)
                raw = (p_even if n < 4 else p_odd)[:, :, :].rearrange("p h t -> p (h t)")
                nc.vector.tensor_tensor(weights[name][1][:, :, :].rearrange("p c d -> p (c d)"),
                                        raw[:, 512 * (n % 4):512 * (n % 4) + 512],
                                        weights[name][0][:, :, :].rearrange("p c d -> p (c d)").bitcast(F32),
                                        ALU.subtract).then_inc(w_lo, 1)
            center(0)
            dve.wait_ge(c_in, 16 * 8)
            dve.wait_ge(consts, 8)
            program(dve, batch)

        @block.gpsimd
        def _(pool):
            nc.gpsimd.memset(ident[:, :], 0.0).then_inc(blank, 1)
            nc.gpsimd.memset(causal[:, :], 0.0).then_inc(blank, 1)
            nc.gpsimd.memset(ident_bf[:, :], 0.0).then_inc(blank, 1)
            pool.wait_ge(blank, 3)
            nc.gpsimd.affine_select(out=ident[:, :], in_=ident[:, :], compare_op=ALU.not_equal, fill=1.0,
                                    base=0, pattern=[[-1, P]], channel_multiplier=1).then_inc(consts, 1)
            nc.gpsimd.affine_select(out=ident_bf[:, :], in_=ident_bf[:, :], compare_op=ALU.not_equal, fill=1.0,
                                    base=0, pattern=[[-1, P]], channel_multiplier=1).then_inc(consts, 1)
            nc.gpsimd.affine_select(out=causal[:, S - P:S], in_=causal[:, S - P:S], compare_op=ALU.is_ge, fill=NEG,
                                    base=0, pattern=[[-1, P]], channel_multiplier=1).then_inc(consts, 1)
            nc.gpsimd.memset(minus_half[:, :], -0.5).then_inc(consts, 1)
            nc.gpsimd.memset(mx[:, :], 0.0).then_inc(consts, 1)
            nc.gpsimd.memset(xnT[:, :, 0:1], 0.0).then_inc(consts, 1)
            for v in v_sb:
                nc.gpsimd.memset(v[:, :, 1, :], 1.0).then_inc(consts, 1)
            pool.wait_ge(c_in, 16 * 8)
            pool.wait_ge(consts, 8)

            def invert(m):
                pool.wait_ge(ln_stats, m + 1)
                nc.gpsimd.tensor_tensor(rstd[:, :], veps[:, :], minus_half[:, :], ALU.pow).then_inc(ln_rstd, 1)

            def batch(b, par):
                attends, front, prev, ahead = flags(b)
                n, npar = b + 1, 1 - par
                for g in range(NG):
                    for s in range(STEPS):
                        here = (g, s)
                        if here == AT["rstd"] and ahead:
                            invert(b + 2)
                        if front:
                            if here == AT["diff"]:
                                pool.wait_ge(xn_hi, DC * (n + 1))
                                pool.wait_ge(y_ready, past(n))
                                nc.gpsimd.tensor_tensor(diff[:, :, :], xnT[:, :, 1:S + 1], xnT[:, :, 0:S],
                                                        ALU.subtract).then_inc(diff_ready, 1)
                            for k, at in enumerate((AT["rope_q_add"], AT["rope_k_add"])):
                                if here == at:
                                    pool.wait_ge(rotated, 2 * n + k + 1)
                                    nc.gpsimd.tensor_tensor(rot[:, 0, :], rot[:, 0, :], tmp[:, 1, :], ALU.subtract)
                                    nc.gpsimd.tensor_tensor(rot[:, 1, :], rot[:, 1, :], tmp[:, 0, :], ALU.add).then_inc(rope_done, 1)
                            for k, (at, parts, loaded) in enumerate(((AT["split_q"], q_parts, q_loaded), (AT["split_k"], k_parts, k_loaded))):
                                if here == at:
                                    pool.wait_ge(qk_hi, 2 * n + k + 1)
                                    for half in range(2):
                                        pool.wait_ge(loaded[half], past((112, 96)[k] * n))
                                    nc.gpsimd.tensor_tensor(parts[:, 1, :, :], rot[:, :, :], parts[:, 0, :, :].bitcast(F32),
                                                            ALU.subtract).then_inc(qk_lo, 1)
                            for k, at in enumerate((AT["mix_k_lo"], AT["mix_r_lo"])):
                                if here == at:
                                    pool.wait_ge(mix_hi, 2 * n + k + 1)
                                    if k == 1:
                                        pool.wait_ge(unit_full, unit_count(b, "K1"))
                                    elif ran(b - 1):
                                        pool.wait_ge(unit_full, unit_count(b - 1, "R1"))
                                    nc.gpsimd.tensor_tensor(b_lo[:, :, :], mix[:, :, :], b_hi[:, :, :].bitcast(F32),
                                                            ALU.subtract).then_inc(mix_lo, 1)
                            if here == AT["ksq_split"]:
                                pool.wait_ge(ksq_hi, n + 1)
                                pool.wait_ge(unit_full, unit_count(b, "O1" if prev else "K1"))
                                nc.gpsimd.tensor_tensor(a_lo[:, :, :], relu_k[:, :, :], a_hi[:, :, :].bitcast(F32),
                                                        ALU.subtract).then_inc(ksq_lo, 1)
                            if here == AT["sigmoid"]:
                                pool.wait_ge(unit_free, unit_count(b, "R1"))
                                pool.sem_inc(gpsimd_passed, 1)
                                nc.gpsimd.tensor_scalar(act_sb[:, :], act_sb[:, :], 0.5, 0.5, ALU.mult, ALU.add).then_inc(r_ready, 1)
                            if here == AT["y_bias"]:
                                pool.wait_ge(y_loaded, 16 * (n + 1))
                                nc.gpsimd.tensor_tensor(y[npar][:, :, :], y[npar][:, :, :],
                                                        bo_sb[:, :].unsqueeze(1).to_broadcast([P, TT, D]), ALU.add).then_inc(y_biased, 1)
                            if here == AT["y_gate"]:
                                pool.wait_ge(y_biased, n + 1)
                                pool.wait_ge(unit_free, unit_count(b, "F1"))
                                nc.gpsimd.tensor_tensor(y[npar][:, :, :], y[npar][:, :, :], r_sb[:, :, :], ALU.add).then_inc(y_ready, 1)
                        if here == AT["attn_split"] and prev:
                            pool.wait_ge(attn_hi, b)
                            pool.wait_ge(unit_full, unit_count(b, "V1") if front else unit_count(b - 1, "F1"))
                            nc.gpsimd.tensor_tensor(a_lo[:, :, :], tmp[:, :, :], a_hi[:, :, :].bitcast(F32),
                                                    ALU.subtract).then_inc(attn_lo, 1)

            invert(0)
            for stack in (k_stack, q_stack):
                nc.gpsimd.memset(stack[:, :, :].bitcast(F32), 0.0).then_inc(zeroed, 1)
            program(pool, batch)


def kernel(**inputs):
    import numpy as _np
    import concourse.bacc as _bacc
    from concourse import mybir as _mybir
    from concourse.bass_utils import run_bass_kernel_spmd as _run

    def get(name):
        return _np.ascontiguousarray(inputs[name])

    half, pair, head = _np.meshgrid(_np.arange(2), _np.arange(8), _np.arange(8), indexing="ij")
    even = ((half * 8 + head) * DK + 2 * pair).ravel()
    perm = _np.concatenate([even, even + 1])
    q, j, d, par = _np.meshgrid(_np.arange(2), _np.arange(4), _np.arange(DK), _np.arange(2), indexing="ij")
    feature = ((GH * (2 * q + par) + j) * DK + d).reshape(P, 2)

    def by_chunk(w):
        return _np.ascontiguousarray(w.T.reshape(DC, P, D).transpose(1, 0, 2))

    inv_freq = (1.0 / _np.float32(10000.0) ** (_np.arange(0, DK, 2, dtype=_np.float32) / _np.float32(DK))).astype(_np.float32)
    angles = _np.arange(S).astype(_np.float32)[None, :] * inv_freq[pair.ravel()][:, None]
    arrays = {
        "x": get("L0_attn_x"),
        "wq": by_chunk(get("L0_attn_Wq")[perm]), "wk": by_chunk(get("L0_attn_Wk")[perm]), "wv": by_chunk(get("L0_attn_Wv")),
        "wo": _np.ascontiguousarray(get("L0_attn_Wo").T[feature]),
        "wr": by_chunk(get("L0_ffn_W_r")), "wf": by_chunk(get("L0_ffn_W_k")), "wc": by_chunk(get("L0_ffn_W_v")),
        "bq": _np.ascontiguousarray(get("L0_attn_bq")[perm].reshape(2, P).T),
        "bk": _np.ascontiguousarray(get("L0_attn_bk")[perm].reshape(2, P).T),
        "bv": get("L0_attn_bv"), "bo": get("L0_attn_bo"),
        "mu_r": _np.ascontiguousarray(get("L0_ffn_mu_r").reshape(DC, P).T),
        "mu_k": _np.ascontiguousarray(get("L0_ffn_mu_k").reshape(DC, P).T),
        "cos_t": _np.cos(angles).astype(_np.float32), "sin_t": _np.sin(angles).astype(_np.float32),
    }
    nc = _bacc.Bacc("TRN2", target_bir_lowering=False, num_devices=1)
    args = {}
    for name, a in arrays.items():
        args[name] = nc.dram_tensor(f"in_{name}", a.shape, _mybir.dt.from_np(a.dtype), kind="ExternalInput").ap()
    out = nc.dram_tensor("out_x", (B, S, D), _mybir.dt.float32, kind="ExternalOutput").ap()
    layer_kernel(nc, **args, out=out)
    r = _run(nc, [{f"in_{name}": a for name, a in arrays.items()}], core_ids=[0])
    return r.results[0]["out_x"]
```

```python
from contextlib import ExitStack

import numpy as np
import concourse.bass as bass
from concourse import mybir

F32 = mybir.dt.float32
F32R = mybir.dt.float32r
BF16 = mybir.dt.bfloat16
ALU = mybir.AluOpType
ACT = mybir.ActivationFunctionType

B, S, D = 32, 512, 256
H, DK = 16, 16
P = 128
TT = S // P
DC = D // P
GH = 4
NG = H // GH
STEPS = 32
MROW = 64
ZROW = 80
GATHER = 16 * 5
Q_DMAS, K_DMAS = 16 * 7, 16 * 6
KROWS = 96
EPS = 1e-5
NEG = -1e30

UNITS = [("T0", 0, 1), ("T1", 0, 10), ("QA", 0, 16), ("QB", 0, 18), ("M0", 0, 21),
         ("KA", 1, 5), ("KB", 1, 10), ("V0", 1, 13), ("V1", 1, 15), ("M1", 1, 19), ("K0", 1, 21), ("K1", 1, 24),
         ("O0", 2, 4), ("O1", 2, 8), ("R0", 2, 11), ("M2", 2, 18), ("R1", 2, 23),
         ("F0", 3, 4), ("F1", 3, 12), ("M3", 3, 22)]

AT = {
    "load_x": (2, 6), "layernorm": (3, 12), "rstd": (3, 9), "center": (3, 22), "diff": (0, 0), "rope_q": (0, 20),
    "rope_q_add": (0, 7), "split_q": (0, 27), "rope_k": (1, 15), "rope_k_add": (1, 15), "split_k": (1, 29),
    "mix_k": (0, 18), "mix_k_hi": (0, 21), "mix_k_lo": (1, 5), "mix_r": (1, 11), "mix_r_hi": (1, 30),
    "mix_r_lo": (2, 4), "square": (2, 4), "ksq_split": (2, 9), "sigmoid": (2, 7), "y_bias": (2, 21),
    "y_gate": (3, 16), "gather1": (0, 16), "load1": (0, 0), "load1_keys": (0, 3), "recip1": (0, 26),
    "spread1": (1, 7), "normalize": (1, 20), "attn_split": (1, 24), "load0": (1, 30), "load0_keys": (2, 2),
    "gather0": (2, 2), "store": (2, 12), "recip0": (2, 16), "spread0": (3, 1), "load_y": (2, 29), "read_T0": (0, 1),
    "read_T1": (0, 10), "read_QA": (0, 16), "high_m0": (0, 24), "low_m0": (0, 23), "send_m0": (0, 25),
    "read_QB": (0, 18), "read_KA": (1, 6), "read_KB": (1, 11), "read_V0": (1, 11), "read_V1": (1, 14),
    "read_K0": (1, 19), "high_m1": (1, 18), "low_m1": (1, 19), "send_m1": (1, 25), "read_K1": (1, 30),
    "read_O0": (2, 3), "read_O1": (2, 9), "read_R0": (2, 13), "high_m2": (2, 16), "low_m2": (2, 27),
    "send_m2": (2, 14), "read_R1": (2, 30), "read_F0": (3, 7), "read_F1": (3, 13), "high_m3": (3, 22),
    "low_m3": (3, 20), "send_m3": (3, 19), "split_q_lo": (0, 24), "split_k_lo": (1, 28), "ksq_split_lo": (2, 5),
    "attn_split_lo": (1, 19),
}

EXP_STEP = [[2, 2, 3, 8, 8, 8, 11, 15, 19, 19, 26, 27],
            [4, 8, 9, 9, 13, 13, 14, 17, 17, 19, 21, 21],
            [4, 4, 6, 6, 10, 11, 12, 14, 16, 20, 23, 25],
            [2, 2, 3, 8, 10, 10, 13, 15, 21, 21, 24, 28]]
AV_STEP = [[14, 21, 23, 33],
           [17, 20, 23, 32],
           [16, 23, 27, 32],
           [15, 22, 31, 33]]
COPY_STEP = [[32],
             [31],
             [41],
             [33]]
MAX_STEP = [[0, 0, 0, 4, 4, 4, 8, 12, 13, 15, 18, 18],
            [0, 0, 0, 2, 5, 7, 7, 8, 10, 14, 14, 14],
            [0, 0, 0, 1, 3, 4, 8, 8, 10, 10, 11, 13],
            [0, 0, 0, 2, 4, 4, 8, 8, 11, 17, 17, 18]]
TURNS = len(MAX_STEP[0])
EXPS = len(EXP_STEP[0])


def due(table, b, g, s, attends, prev):
    found = []
    for late in (1, 0):
        if attends if g >= late else prev:
            found += [(NG * b + g - late, (g - late) % NG, item)
                      for item, at in enumerate(table[(g - late) % NG]) if at == s + STEPS * late]
    return found


def has(unit, b):
    if unit[0] == "M":
        return 0 <= 4 * b + int(unit[1]) + 1 < NG * B
    if unit[0] == "O":
        return b >= 1
    return b + 1 < B


def unit_count(b, unit):
    names = [u for u, _, _ in UNITS]
    if isinstance(b, int):
        before = sum(has(u, a) for a in range(-1, b) for u in names)
        return before + sum(has(u, b) for u in names[:names.index(unit) + 1])
    first = sum(has(u, a) for a in (-1, 0) for u in names)
    return b * len(names) + (first - len(names) + names.index(unit) + 1)


def ran(b):
    return not isinstance(b, int) or b >= -1


def past(count):
    return max(count, 0) if isinstance(count, int) else count


def layer_kernel(nc, x, wq, wk, wv, wo, wr, wf, wc, bq, bk, bv, bo, mu_r, mu_k, cos_t, sin_t, out):
    with ExitStack() as ctx:
        def sb(name, shape, dt=F32):
            return ctx.enter_context(nc.sbuf_tensor(name, shape, dt))

        def psum(name, shape):
            return ctx.enter_context(nc.psum_tensor(name, shape, F32))

        def sem(name):
            return ctx.enter_context(nc.semaphore(name))

        max_ps = psum("max_ps", [P, 3, S])
        exp_ps = psum("exp_ps", [P, 3, S])
        av_ps = psum("av_ps", [P, S])
        unit_ps = psum("unit_ps", [P, S])

        weights = {}
        for name in ("q", "k", "v", "o", "r", "f", "c"):
            weights[name] = [sb(f"w{name}_{part}", [P, DC, D], F32R) for part in ("hi", "lo")]
        cos_sb, sin_sb = sb("cos_sb", [P, S]), sb("sin_sb", [P, S])
        ident, ident_bf = sb("ident", [P, P]), sb("ident_bf", [P, P], BF16)
        causal = sb("causal", [P, S], BF16)
        bias_q, bias_k = sb("bias_q", [P, 2]), sb("bias_k", [P, 2])
        mur_sb, muk_sb = sb("mur_sb", [P, DC]), sb("muk_sb", [P, DC])
        bv_sb, bo_sb = sb("bv_sb", [P, D]), sb("bo_sb", [P, D])
        minus_half = sb("minus_half", [P, TT])

        q_stack, k_stack = sb("q_stack", [KROWS, H, S], F32R), sb("k_stack", [KROWS, H, S], F32R)
        p_first = sb("p_first", [P, GH, S])
        p_odd = sb("p_odd", [P, GH, S - P])
        p_third = sb("p_third", [P, GH, S - 2 * P])
        v_sb = [sb(f"v{i}", [P, TT * H, 2, DK]) for i in range(2)]
        mx = sb("mx", [P, 2 * GH * TT])
        negm_hi, negm_lo = sb("negm_hi", [GH * TT, P], F32R), sb("negm_lo", [GH * TT, P], F32R)
        av_sb = sb("av_sb", [P, 2, S])
        num = sb("num", [P, 2, S])
        sums = sb("sums", [P, 64])
        rec = sb("rec", [P, 2, S])
        rscratch = nc.dram_tensor("rscratch", (2, GH, 2, S), F32, kind="Internal").ap()

        x_in = sb("x_in", [P, TT, D])
        stats, mv = sb("stats", [P, TT, 6]), sb("mv", [P, TT, 2])
        veps, rstd = sb("veps", [P, TT]), sb("rstd", [P, TT])
        xnT = sb("xnT", [P, DC, S + 1])
        a_hi, a_lo = sb("a_hi", [P, DC, S], F32R), sb("a_lo", [P, DC, S], F32R)
        b_hi, b_lo = sb("b_hi", [P, DC, S], F32R), sb("b_lo", [P, DC, S], F32R)
        mix = x_in[:, :, :].rearrange("p a d -> p (a d)").rearrange("p (c t) -> p c t", c=DC)
        act_sb = sb("act_sb", [P, DC * S])
        diff = act_sb[:, :].rearrange("p (c t) -> p c t", c=DC)
        relu_k = diff
        r_sb = act_sb[:, :].rearrange("p (a d) -> p a d", a=TT)
        rot = sb("rot", [P, 2, S])
        tmp = sb("tmp", [P, 2, S])
        q_parts, k_parts = sb("q_parts", [P, 2, 2, S], F32R), sb("k_parts", [P, 2, 2, S], F32R)
        y = [sb(f"y{i}", [P, TT, D]) for i in range(2)]

        w_in, c_in = sem("w_in"), sem("c_in")
        w_hi, w_lo, consts, zeroed, ones, blank = (sem(n) for n in ("w_hi", "w_lo", "consts", "zeroed", "ones", "blank"))
        unit_full, unit_free = sem("unit_full"), sem("unit_free")
        max_full, max_done = sem("max_full"), sem("max_done")
        exp_full, exp_done = sem("exp_full"), sem("exp_done")
        av_done, av_copied = sem("av_done"), sem("av_copied")
        negm_ready, m_rows = sem("negm_ready"), sem("m_rows")
        q_loaded = [sem(f"q_loaded{i}") for i in range(2)]
        k_loaded = [sem(f"k_loaded{i}") for i in range(2)]
        gathered, recip_done, r_written, r_read = sem("gathered"), sem("recip_done"), sem("r_written"), sem("r_read")
        attn_ready, attn_hi, attn_lo = sem("attn_ready"), sem("attn_hi"), sem("attn_lo")
        stored = sem("stored")
        x_loaded, y_loaded, y_biased, y_ready = sem("x_loaded"), sem("y_loaded"), sem("y_biased"), sem("y_ready")
        ln_step, ln_stats, ln_rstd, xn_ready = sem("ln_step"), sem("ln_stats"), sem("ln_rstd"), sem("xn_ready")
        xn_hi, diff_ready = sem("xn_hi"), sem("diff_ready")
        mixed, mix_hi, mix_lo = sem("mixed"), sem("mix_hi"), sem("mix_lo")
        sin_done, rotated, rope_done, qk_hi, qk_lo = (sem(n) for n in ("sin_done", "rotated", "rope_done", "qk_hi", "qk_lo"))
        ksq, ksq_hi, ksq_lo, r_ready = sem("ksq"), sem("ksq_hi"), sem("ksq_lo"), sem("r_ready")

        sync_passed, vector_passed, gpsimd_passed = sem("sync_passed"), sem("vector_passed"), sem("gpsimd_passed")

        def p_of(kt):
            return (p_first, p_odd, p_third, p_odd)[kt][:, :, 0:S - P * kt]

        def program(eng, batch):
            batch(-1, 1)
            batch(0, 0)
            with eng.Fori(0, (B - 4) // 2) as i:
                batch(2 * i + 1, 1)
                batch(2 * i + 2, 0)
            for b in range(B - 3, B + 1):
                batch(b, b % 2)

        def flags(b):
            if isinstance(b, int):
                return 0 <= b < B, b + 1 < B, b >= 1, b + 2 < B
            return True, True, True, True

        def next_group(b, g):
            return not isinstance(b, int) or 0 <= NG * b + g + 1 < NG * B

        EXP_UNITS = [(kt, h, h + 1) for kt in (0, 1) for h in range(GH)] + [(kt, h, h + 2) for kt in (2, 3) for h in (0, 2)]
        LAST_UNIT = [4, 8, 10, 12]
        TURN_TILES = [(0, 1), (2,), (3,)]

        def exp_view(u):
            kt, bank = EXP_UNITS[u][0], exp_ps[:, u % 3, :]
            if kt < 2:
                return bank[:, 0:S - P * kt].unsqueeze(1)
            return bank.rearrange("p (h t) -> p h t", h=2)

        block = ctx.enter_context(nc.Block())

        @block.sync
        def _(sp):
            x_tiles = x.rearrange("b (a p) d -> b p a d", p=P)
            out_tiles = out.rearrange("b (a p) d -> b p a d", p=P)

            def row(ap, b):
                return ap[b] if isinstance(b, int) else ap[bass.ds(b, 1)].rearrange("o p a d -> p (o a) d")

            sp.dma_start(x_in[:, :, :], row(x_tiles, 0)).then_inc(x_loaded, 16)
            for n, (name, w) in enumerate((("q", wq), ("k", wk), ("v", wv), ("o", wo), ("r", wr), ("f", wf), ("c", wc))):
                raw = (p_first if n < 4 else p_odd)[:, :, :].rearrange("p h t -> p (h t)")
                sp.dma_start(raw[:, 512 * (n % 4):512 * (n % 4) + 512], w.rearrange("p c d -> p (c d)")).then_inc(w_in, 16)
            for dst, src in ((cos_sb, cos_t), (sin_sb, sin_t), (bias_q, bq), (bias_k, bk), (mur_sb, mu_r), (muk_sb, mu_k)):
                sp.dma_start(dst[:, :], src).then_inc(c_in, 16)
            for dst, src in ((bv_sb, bv), (bo_sb, bo)):
                sp.dma_start(dst[:, :], src.unsqueeze(0).to_broadcast([P, D])).then_inc(c_in, 16)

            def stack_rows(stack, first, rows, head, heads):
                return stack[first:first + rows, head:head + heads, :].rearrange("r h t -> r (h t)").bitcast(F32)

            def load_stack(stack, parts, order, half, loaded):
                for term, part in enumerate(order):
                    for ab in range(2):
                        first = 16 * term + 8 * ab
                        sp.dma_start(stack_rows(stack, first, 8, 8 * half, 8),
                                     parts[64 * half:64 * half + 64, part, ab, :].bitcast(F32)).then_inc(loaded, 16)

            def load_queries(n, half):
                sp.wait_ge(qk_hi, 2 * n + 1)
                sp.sem_inc(sync_passed, 1)
                sp.wait_ge(qk_lo, 2 * n + 1)
                sp.sem_inc(sync_passed, 1)
                load_stack(q_stack, q_parts, (0, 1, 0), half, q_loaded[half])
                sp.dma_start(stack_rows(q_stack, MROW, 2, 8 * half, 8), stack_rows(q_stack, ZROW, 2, 8 * half, 8)).then_inc(q_loaded[half], 16)

            def load_keys(n, half):
                sp.wait_ge(qk_hi, 2 * n + 2)
                sp.sem_inc(sync_passed, 1)
                sp.wait_ge(qk_lo, 2 * n + 2)
                sp.sem_inc(sync_passed, 1)
                load_stack(k_stack, k_parts, (0, 0, 1), half, k_loaded[half])

            def gather(b, q):
                pair = 2 * b + q
                sp.wait_ge(av_copied, 2 * (pair + 1))
                sp.sem_inc(sync_passed, 1)
                sp.wait_ge(attn_ready, past(b))
                sp.sem_inc(sync_passed, 1)
                sp.wait_ge(r_written, past(16 * (pair - 1)))
                sp.sem_inc(sync_passed, 1)
                for j in range(GH):
                    sp.dma_start(num[64 * q + 16 * j:64 * q + 16 * j + 16, :, :],
                                 av_sb[32 * j:32 * j + 16, :, :]).then_inc(gathered, 16)
                sp.dma_start(sums[64 * q:64 * q + 64, :], av_sb[16:P:32, :, :]).then_inc(gathered, 16)

            def spread(b, q):
                pair = 2 * b + q
                sp.wait_ge(recip_done, pair + 1)
                sp.sem_inc(sync_passed, 1)
                sp.wait_ge(r_read, past(16 * (pair - 1)))
                sp.sem_inc(sync_passed, 1)
                sp.wait_ge(attn_ready, past(b))
                sp.dma_start(rscratch[q].rearrange("h g (a t) -> (h g a) t", a=8), sums[64 * q:64 * q + 64, :]).then_inc(r_written, 16)
                sp.wait_ge(r_written, 16 * (pair + 1))
                sp.sem_inc(sync_passed, 1)
                sp.dma_start(rec[64 * q:64 * q + 64, :, :],
                             rscratch[q].unsqueeze(1).to_broadcast([GH, DK, 2, S])).then_inc(r_read, 16)

            def batch(b, par):
                attends, front, prev, ahead = flags(b)
                n, ypar = b + 1, 1 - par
                for g in range(NG):
                    for s in range(STEPS):
                        if (g, s) == AT["load_x"] and ahead:
                            sp.wait_ge(mix_hi, 2 * n + 2)
                            sp.sem_inc(sync_passed, 1)
                            sp.wait_ge(mix_lo, 2 * n + 2)
                            sp.dma_start(x_in[:, :, :], row(x_tiles, b + 2)).then_inc(x_loaded, 16)
                        if (g, s) == AT["gather1"] and prev:
                            gather(b - 1, 1)
                        if (g, s) == AT["load1"] and attends:
                            sp.wait_ge(exp_full, past(NG * EXPS * b))
                            sp.sem_inc(sync_passed, 1)
                            load_queries(b, 1)
                        if (g, s) == AT["load1_keys"] and attends:
                            sp.wait_ge(exp_full, past(NG * EXPS * b))
                            sp.sem_inc(sync_passed, 1)
                            load_keys(b, 1)
                        if (g, s) == AT["gather0"] and attends:
                            gather(b, 0)
                        if (g, s) == AT["load0"] and front:
                            sp.wait_ge(exp_full, past(EXPS * (NG * b + 2)))
                            sp.sem_inc(sync_passed, 1)
                            load_queries(n, 0)
                        if (g, s) == AT["load0_keys"] and front:
                            sp.wait_ge(exp_full, past(EXPS * (NG * b + 2)))
                            sp.sem_inc(sync_passed, 1)
                            load_keys(n, 0)
                        if (g, s) == AT["store"] and prev:
                            sp.wait_ge(unit_free, unit_count(b, "O1"))
                            sp.dma_start(row(out_tiles, b - 1), y[ypar][:, :, :]).then_inc(stored, 16)
                        if (g, s) == AT["load_y"] and front:
                            sp.wait_ge(stored, past(16 * (b if prev else 0)))
                            sp.dma_start(y[ypar][:, :, :], row(x_tiles, n)).then_inc(y_loaded, 16)
                        for m in range(NG):
                            if (g, s) == AT[f"send_m{m}"] and next_group(b, m):
                                nxt = NG * b + m + 1
                                h0 = (GH * (m + 1)) % H
                                sp.wait_ge(negm_ready, nxt + 1)
                                sp.dma_start(stack_rows(q_stack, MROW, 1, h0, GH), negm_hi[:, :].bitcast(F32)).then_inc(m_rows, 16)
                                sp.wait_ge(unit_free, unit_count(b, f"M{m}"))
                                sp.dma_start(stack_rows(q_stack, MROW + 1, 1, h0, GH), negm_lo[:, :].bitcast(F32)).then_inc(m_rows, 16)
                        if (g, s) == AT["spread1"] and prev:
                            spread(b - 1, 1)
                        if (g, s) == AT["spread0"] and attends:
                            spread(b, 0)

            sp.wait_ge(consts, 8)
            sp.wait_ge(zeroed, 2)
            sp.dma_start(stack_rows(k_stack, MROW, 2, 0, H), v_sb[0][:, 0:2 * H * S // P // DK, 1, :]).then_inc(ones, 16)
            sp.wait_ge(ones, 16)
            program(sp, batch)
            sp.wait_ge(stored, 16 * B)

        @block.tensor
        def _(pe):
            pe.wait_ge(consts, 8)
            pe.wait_ge(w_hi, 7)
            pe.wait_ge(w_lo, 7)

            def claim(b, unit):
                pe.wait_ge(unit_free, past(unit_count(b, unit) - 1))

            def project(hi_lo, w, token_tiles=None, cols=None):
                terms = [(c, i, j) for c in range(DC) for i, j in ((0, 0), (0, 1), (1, 0))]
                if token_tiles is None:
                    for m, (c, i, j) in enumerate(terms):
                        last = nc.tensor.matmul(unit_ps[:, :], weights[w][j][:, c, cols:cols + P], hi_lo[i][:, c, :],
                                                start=m == 0, stop=m == 5)
                else:
                    for k, a in enumerate(token_tiles):
                        for m, (c, i, j) in enumerate(terms):
                            last = nc.tensor.matmul(unit_ps[:, D * k:D * k + D], hi_lo[i][:, c, P * a:P * a + P],
                                                    weights[w][j][:, c, :], start=m == 0, stop=m == 5)
                last.then_inc(unit_full, 1)

            def unit(b, name):
                claim(b, name)
                n, kind, k = b + 1, name[0], name[1:]
                if kind == "T":
                    pe.wait_ge(xn_ready, n + 1)
                    for a in range(TT):
                        last = nc.tensor.transpose(unit_ps[:, P * a:P * a + P], x_in[:, a, P * int(k):P * int(k) + P], ident[:, :])
                    last.then_inc(unit_full, 1)
                elif name in ("QA", "QB", "KA", "KB"):
                    project((a_hi, a_lo), kind.lower(), cols=P * "AB".index(k))
                elif kind == "V":
                    project((a_hi, a_lo), "v", token_tiles=(2 * int(k), 2 * int(k) + 1))
                elif kind == "K":
                    pe.wait_ge(mix_hi, 2 * n + 1)
                    pe.wait_ge(mix_lo, 2 * n + 1)
                    project((b_hi, b_lo), "f", cols=P * int(k))
                elif kind == "R":
                    pe.wait_ge(mix_hi, 2 * n + 2)
                    pe.wait_ge(mix_lo, 2 * n + 2)
                    project((b_hi, b_lo), "r", token_tiles=(2 * int(k), 2 * int(k) + 1))
                elif kind == "F":
                    pe.wait_ge(ksq_hi, n + 1)
                    pe.wait_ge(ksq_lo, n + 1)
                    project((a_hi, a_lo), "c", token_tiles=(2 * int(k), 2 * int(k) + 1))
                elif kind == "O":
                    pe.wait_ge(attn_hi, b)
                    pe.wait_ge(attn_lo, b)
                    project((a_hi, a_lo), "o", token_tiles=(2 * int(k), 2 * int(k) + 1))
                elif kind == "M":
                    pe.wait_ge(max_done, TURNS * (NG * b + int(k) + 2))
                    nc.tensor.transpose(unit_ps[0:2 * GH * TT, 0:P], mx[:, :], ident[:, :]).then_inc(unit_full, 1)

            def max_scores(b, g, turn):
                nxt = TURNS * (NG * b + g + 1) + turn
                h, tiles = (GH * (g + 1)) % H + turn // 3, TURN_TILES[turn % 3]
                if turn == 0:
                    half = h // 8
                    nb = b + 1 if g == NG - 1 else b
                    pe.wait_ge(q_loaded[half], Q_DMAS * (nb + 1))
                    pe.wait_ge(k_loaded[half], K_DMAS * (nb + 1))
                pe.wait_ge(max_done, past(nxt - 2))
                for i, qt in enumerate(tiles):
                    keys = max(2 * P, P * (qt + 1))
                    last = nc.tensor.matmul(max_ps[:, turn % 3, 2 * P * i:2 * P * i + keys], q_stack[:, h, P * qt:P * qt + P],
                                            k_stack[:, h, 0:keys], start=True, stop=True)
                last.then_inc(max_full, 1)

            def exp_scores(group, g, u):
                kt, h0, h1 = EXP_UNITS[u]
                if u == 0:
                    pe.wait_ge(m_rows, 32 * (group + 1))
                pe.wait_ge(exp_done, past(EXPS * group + u - 2))
                view = exp_view(u)
                q0 = min(P * kt, S - 2 * P)
                for h in range(h0, h1):
                    nc.tensor.matmul(view[:, h - h0, :], k_stack[:, GH * g + h, P * kt:P * kt + P],
                                     q_stack[:, GH * g + h, q0:S], start=True, stop=False)
                    last = nc.tensor.matmul(view[:, h - h0, P * kt - q0:P * kt - q0 + P], causal[:, S - P:S], ident_bf[:, :],
                                            start=False, stop=True)
                last.then_inc(exp_full, 1)

            def attend(group, b, par, g, kt):
                pe.wait_ge(exp_done, EXPS * group + LAST_UNIT[kt])
                if kt == 0:
                    pe.wait_ge(av_copied, past(group))
                    if g == 0:
                        pe.wait_ge(unit_free, unit_count(b - 1, "F1"))
                p = p_of(kt)
                for j in range(GH):
                    last = nc.tensor.matmul(av_ps[32 * j:32 * j + 32, P * kt:S],
                                            v_sb[par][:, kt * H + GH * g + j, :, :].rearrange("p x d -> p (x d)"),
                                            p[:, j, :], start=kt == 0, stop=kt == TT - 1)
                last.then_inc(av_done, 1)

            def batch(b, par):
                attends, front, prev, ahead = flags(b)
                for g in range(NG):
                    for s in range(STEPS):
                        for group, g2, u in due(EXP_STEP, b, g, s, attends, prev):
                            exp_scores(group, g2, u)
                        if next_group(b, g):
                            for turn, at in enumerate(MAX_STEP[g]):
                                if at == s:
                                    max_scores(b, g, turn)
                        for group, g2, kt in due(AV_STEP, b, g, s, attends, prev):
                            attend(group, b, par if g2 <= g else 1 - par, g2, kt)
                        for name, ug, us in UNITS:
                            if (g, s) == (ug, us) and (not isinstance(b, int) or has(name, b)):
                                unit(b, name)

            program(pe, batch)

        @block.scalar
        def _(act):
            def split_weight(n, name):
                act.wait_ge(w_in, 16 * 7)
                raw = (p_first if n < 4 else p_odd)[:, :, :].rearrange("p h t -> p (h t)")
                nc.scalar.activation(weights[name][0][:, :, :].rearrange("p c d -> p (c d)"),
                                     raw[:, 512 * (n % 4):512 * (n % 4) + 512], ACT.Copy).then_inc(w_hi, 1)

            for n, name in enumerate(("q", "k", "v", "o", "r", "f", "c")):
                split_weight(n, name)
            act.wait_ge(w_lo, 7)
            act.wait_ge(c_in, 16 * 8)
            act.wait_ge(consts, 8)

            def batch(b, par):
                attends, front, prev, ahead = flags(b)
                n = b + 1
                for g in range(NG):
                    for s in range(STEPS):
                        here = (g, s)
                        for group, g2, u in due(EXP_STEP, b, g, s, attends, prev):
                            kt, h0, h1 = EXP_UNITS[u]
                            act.wait_ge(exp_full, EXPS * group + u + 1)
                            if u == 0:
                                act.wait_ge(av_done, past(4 * group - 3))
                            if u == 4:
                                act.wait_ge(av_done, past(4 * group))
                            if u == 8:
                                act.wait_ge(av_done, past(4 * group - 1))
                            if u == 10:
                                act.wait_ge(av_done, 4 * group + 2)
                            view = exp_view(u)
                            valid = S - P * kt
                            view = view[:, :, view.shape[2] - valid:]
                            nc.scalar.activation(p_of(kt)[:, h0:h1, :], view, ACT.Exp, scale=DK ** -0.5).then_inc(exp_done, 1)
                        for group, g2, _ in due(COPY_STEP, b, g, s, attends, prev):
                            act.wait_ge(av_done, 4 * (group + 1))
                            act.wait_ge(gathered, past(GATHER * (2 * b + (g2 if g2 <= g else g2 - NG) // 2)))
                            nc.scalar.activation(av_sb[:, g2 % 2, :], av_ps[:, :], ACT.Copy).then_inc(av_copied, 1)
                        for m in range(NG):
                            if (g, s) == AT[f"high_m{m}"] and next_group(b, m):
                                act.wait_ge(unit_full, unit_count(b, f"M{m}"))
                                act.wait_ge(m_rows, past(32 * (NG * b + m + 1)))
                                nc.scalar.activation(negm_hi[:, :], unit_ps[0:GH * TT, 0:P], ACT.Copy, scale=-1.0).then_inc(negm_ready, 1)
                        if front:
                            for c in range(DC):
                                if here == AT[f"read_T{c}"]:
                                    act.wait_ge(unit_full, unit_count(b, f"T{c}"))
                                    if c == 0:
                                        act.wait_ge(mixed, past(2 * n))
                                        if ran(b - 1):
                                            act.wait_ge(unit_full, unit_count(b - 1, "F1"))
                                    nc.scalar.activation(a_hi[:, c, :], unit_ps[:, :], ACT.Copy)
                                    nc.scalar.activation(xnT[:, c, 1:S + 1], unit_ps[:, :], ACT.Copy).then_inc(xn_hi, 1)
                            for name, bias in (("QA", bias_q), ("QB", bias_q), ("KA", bias_k), ("KB", bias_k)):
                                if here == AT[f"read_{name}"]:
                                    ab = "AB".index(name[1])
                                    act.wait_ge(unit_full, unit_count(b, name))
                                    if ab == 0:
                                        act.wait_ge(qk_lo, past(2 * n + (name[0] == "K")))
                                        act.wait_ge(qk_hi, past(2 * n + (name[0] == "K")))
                                    nc.scalar.activation(rot[:, ab, :], unit_ps[:, :], ACT.Identity, bias=bias[:, ab:ab + 1]).then_inc(unit_free, 1)
                            for k, (at, parts, half1) in enumerate(((AT["split_q"], q_parts, q_loaded), (AT["split_k"], k_parts, k_loaded))):
                                if here == at:
                                    act.wait_ge(rope_done, 2 * n + k + 1)
                                    for half in range(2):
                                        act.wait_ge(half1[half], past((Q_DMAS, K_DMAS)[k] * n))
                                    nc.scalar.activation(parts[:, 0, :, :], rot[:, :, :], ACT.Copy).then_inc(qk_hi, 1)
                            for k, at in enumerate((AT["mix_k_hi"], AT["mix_r_hi"])):
                                if here == at:
                                    act.wait_ge(mixed, 2 * n + k + 1)
                                    if k == 1:
                                        act.wait_ge(unit_full, unit_count(b, "K1"))
                                    elif ran(b - 1):
                                        act.wait_ge(unit_full, unit_count(b - 1, "R1"))
                                    nc.scalar.activation(b_hi[:, :, :], mix[:, :, :], ACT.Copy).then_inc(mix_hi, 1)
                            for c, at in enumerate((AT["read_K0"], AT["read_K1"])):
                                if here == at:
                                    act.wait_ge(unit_full, unit_count(b, f"K{c}"))
                                    act.wait_ge(mixed, 2 * n + 2)
                                    nc.scalar.activation(relu_k[:, c, :], unit_ps[:, :], ACT.Relu).then_inc(unit_free, 1)
                            if here == AT["square"]:
                                act.wait_ge(unit_free, unit_count(b, "K1"))
                                nc.scalar.activation(relu_k[:, :, :], relu_k[:, :, :], ACT.Square).then_inc(ksq, 1)
                            if here == AT["ksq_split"]:
                                act.wait_ge(ksq, n + 1)
                                act.wait_ge(unit_full, unit_count(b, "O1" if prev else "K1"))
                                nc.scalar.activation(a_hi[:, :, :], relu_k[:, :, :], ACT.Copy).then_inc(ksq_hi, 1)
                            for k, at in enumerate((AT["read_R0"], AT["read_R1"])):
                                if here == at:
                                    act.wait_ge(unit_full, unit_count(b, f"R{k}"))
                                    act.wait_ge(ksq_lo, n + 1)
                                    act.wait_ge(ksq_hi, n + 1)
                                    nc.scalar.activation(r_sb[:, 2 * k:2 * k + 2, :].rearrange("p a d -> p (a d)"),
                                                         unit_ps[:, :], ACT.Tanh, scale=0.5).then_inc(unit_free, 1)
                        if here == AT["attn_split"] and prev:
                            act.wait_ge(attn_ready, b)
                            act.wait_ge(unit_full, unit_count(b, "V1") if front else unit_count(b - 1, "F1"))
                            nc.scalar.activation(a_hi[:, :, :], tmp[:, :, :], ACT.Copy).then_inc(attn_hi, 1)

            program(act, batch)

        @block.vector
        def _(dve):
            def statistics(m):
                dve.wait_ge(x_loaded, 16 * (m + 1))
                dve.wait_ge(xn_ready, m)
                for a in range(TT):
                    nc.vector.bn_stats(stats[:, a, :], x_in[:, a, :]).then_inc(ln_step, 1)
                dve.wait_ge(ln_step, (TT + 1) * m + TT)
                dve.sem_inc(vector_passed, 1)
                for a in range(TT):
                    last = nc.vector.bn_aggr(mv[:, a, :], stats[:, a, :])
                last.then_inc(ln_step, 1)
                dve.wait_ge(ln_step, (TT + 1) * (m + 1))
                nc.vector.tensor_scalar(veps[:, :], mv[:, :, 1], EPS, None, ALU.add).then_inc(ln_stats, 1)

            def center(m):
                dve.wait_ge(ln_rstd, m + 1)
                for a in range(TT):
                    last = nc.vector.tensor_scalar(x_in[:, a, :], x_in[:, a, :], mv[:, a, 0:1], rstd[:, a:a + 1],
                                                   ALU.subtract, ALU.mult)
                last.then_inc(xn_ready, 1)

            def batch(b, par):
                attends, front, prev, ahead = flags(b)
                n, npar = b + 1, 1 - par
                for g in range(NG):
                    for s in range(STEPS):
                        here = (g, s)
                        if here == AT["layernorm"] and ahead:
                            statistics(b + 2)
                        if here == AT["center"] and ahead:
                            center(b + 2)
                        for turn, at in enumerate(MAX_STEP[g]):
                            if at == s and next_group(b, g):
                                if turn == 0:
                                    if g > 0:
                                        dve.wait_ge(unit_full, unit_count(b, f"M{g - 1}"))
                                    elif ran(b - 1):
                                        dve.wait_ge(unit_full, unit_count(b - 1, "M3"))
                                dve.wait_ge(max_full, TURNS * (NG * b + g + 1) + turn + 1)
                                dve.sem_inc(vector_passed, 1)
                                for i, qt in enumerate(TURN_TILES[turn % 3]):
                                    keys, col, u = P * (qt + 1), 2 * P * i, TT * (turn // 3) + qt
                                    last = nc.vector.tensor_tensor_reduce(out=max_ps[:, turn % 3, col:col + keys],
                                                                          in0=max_ps[:, turn % 3, col:col + keys],
                                                                          in1=causal[:, S - keys:S], scale=1.0, scalar=NEG,
                                                                          op0=ALU.add, op1=ALU.max, accum_out=mx[:, u:u + 1])
                                last.then_inc(max_done, 1)
                        for m in range(NG):
                            if (g, s) == AT[f"low_m{m}"] and next_group(b, m):
                                dve.wait_ge(negm_ready, NG * b + m + 2)
                                nc.vector.scalar_tensor_tensor(negm_lo[:, :], unit_ps[0:GH * TT, 0:P], -1.0,
                                                               negm_hi[:, :].bitcast(F32), ALU.mult, ALU.subtract).then_inc(unit_free, 1)
                        if front:
                            for k, (at, mu) in enumerate(((AT["mix_k"], muk_sb), (AT["mix_r"], mur_sb))):
                                if here == at:
                                    dve.wait_ge(diff_ready, n + 1)
                                    dve.wait_ge(mix_hi, past(2 * n + k))
                                    dve.wait_ge(mix_lo, past(2 * n + k))
                                    for c in range(DC):
                                        last = nc.vector.scalar_tensor_tensor(mix[:, c, :], diff[:, c, :], mu[:, c:c + 1],
                                                                              xnT[:, c, 0:S], ALU.mult, ALU.add)
                                    last.then_inc(mixed, 1)
                            for k, (at, name) in enumerate(((AT["rope_q"], "QB"), (AT["rope_k"], "KB"))):
                                if here == at:
                                    dve.wait_ge(unit_free, unit_count(b, name))
                                    dve.wait_ge(rope_done, past(2 * n + k))
                                    if k == 0 and prev:
                                        dve.wait_ge(attn_lo, b - 1)
                                        dve.wait_ge(attn_hi, b - 1)
                                    nc.vector.tensor_tensor(tmp[:, :, :], rot[:, :, :], sin_sb[:, :].unsqueeze(1).to_broadcast([P, 2, S]),
                                                            ALU.mult).then_inc(sin_done, 1)
                                    dve.wait_ge(sin_done, 2 * n + k + 1)
                                    nc.vector.tensor_tensor(rot[:, :, :], rot[:, :, :], cos_sb[:, :].unsqueeze(1).to_broadcast([P, 2, S]),
                                                            ALU.mult).then_inc(rotated, 1)
                            for c in range(DC):
                                if here == AT[f"read_T{c}"]:
                                    dve.wait_ge(xn_hi, DC * n + c + 1)
                                    if ran(b - 1):
                                        dve.wait_ge(unit_full, unit_count(b - 1, "F1"))
                                    nc.vector.tensor_tensor(a_lo[:, c, :], unit_ps[:, :], a_hi[:, c, :].bitcast(F32),
                                                            ALU.subtract).then_inc(unit_free, 1)
                            for k, at in enumerate((AT["read_V0"], AT["read_V1"])):
                                if here == at:
                                    dve.wait_ge(unit_full, unit_count(b, f"V{k}"))
                                    dve.wait_ge(av_done, past(16 * (b if prev else 0)))
                                    for a in range(2):
                                        kt = 2 * k + a
                                        last = nc.vector.tensor_tensor(
                                            v_sb[npar][:, kt * H:(kt + 1) * H, 0, :],
                                            unit_ps[:, D * a:D * a + D].rearrange("p (h d) -> p h d", d=DK),
                                            bv_sb[:, :].rearrange("p (h d) -> p h d", d=DK), ALU.add)
                                    last.then_inc(unit_free, 1)
                            for k, at in enumerate((AT["read_F0"], AT["read_F1"])):
                                if here == at:
                                    dve.wait_ge(unit_full, unit_count(b, f"F{k}"))
                                    dve.wait_ge(r_ready, n + 1)
                                    half = r_sb[:, 2 * k:2 * k + 2, :].rearrange("p a d -> p (a d)")
                                    nc.vector.tensor_tensor(half, half, unit_ps[:, :], ALU.mult).then_inc(unit_free, 1)
                        for at, ok, pair, q in ((AT["recip1"], prev, 2 * b - 1, 1), (AT["recip0"], attends, 2 * b, 0)):
                            if here == at and ok:
                                dve.wait_ge(gathered, GATHER * (pair + 1))
                                nc.vector.reciprocal(sums[64 * q:64 * q + 64, :], sums[64 * q:64 * q + 64, :]).then_inc(recip_done, 1)
                        if here == AT["normalize"] and prev:
                            dve.wait_ge(r_read, 16 * 2 * b)
                            if front:
                                dve.wait_ge(rope_done, 2 * n + 2)
                            nc.vector.tensor_tensor(tmp[:, :, :], num[:, :, :], rec[:, :, :], ALU.mult).then_inc(attn_ready, 1)
                        for k, at in enumerate((AT["read_O0"], AT["read_O1"])):
                            if here == at and prev:
                                dve.wait_ge(unit_full, unit_count(b, f"O{k}"))
                                dve.wait_ge(y_ready, b)
                                half = y[npar][:, 2 * k:2 * k + 2, :].rearrange("p a d -> p (a d)")
                                nc.vector.tensor_tensor(half, unit_ps[:, :], half, ALU.add).then_inc(unit_free, 1)

            statistics(0)
            for n, name in enumerate(("q", "k", "v", "o", "r", "f", "c")):
                dve.wait_ge(w_hi, n + 1)
                raw = (p_first if n < 4 else p_odd)[:, :, :].rearrange("p h t -> p (h t)")
                nc.vector.tensor_tensor(weights[name][1][:, :, :].rearrange("p c d -> p (c d)"),
                                        raw[:, 512 * (n % 4):512 * (n % 4) + 512],
                                        weights[name][0][:, :, :].rearrange("p c d -> p (c d)").bitcast(F32),
                                        ALU.subtract).then_inc(w_lo, 1)
            center(0)
            dve.wait_ge(c_in, 16 * 8)
            dve.wait_ge(consts, 8)
            program(dve, batch)

        @block.gpsimd
        def _(pool):
            nc.gpsimd.memset(ident[:, :], 0.0).then_inc(blank, 1)
            nc.gpsimd.memset(causal[:, :], 0.0).then_inc(blank, 1)
            nc.gpsimd.memset(ident_bf[:, :], 0.0).then_inc(blank, 1)
            pool.wait_ge(blank, 3)
            nc.gpsimd.affine_select(out=ident[:, :], in_=ident[:, :], compare_op=ALU.not_equal, fill=1.0,
                                    base=0, pattern=[[-1, P]], channel_multiplier=1).then_inc(consts, 1)
            nc.gpsimd.affine_select(out=ident_bf[:, :], in_=ident_bf[:, :], compare_op=ALU.not_equal, fill=1.0,
                                    base=0, pattern=[[-1, P]], channel_multiplier=1).then_inc(consts, 1)
            nc.gpsimd.affine_select(out=causal[:, S - P:S], in_=causal[:, S - P:S], compare_op=ALU.is_ge, fill=NEG,
                                    base=0, pattern=[[-1, P]], channel_multiplier=1).then_inc(consts, 1)
            nc.gpsimd.memset(minus_half[:, :], -0.5).then_inc(consts, 1)
            nc.gpsimd.memset(mx[:, :], 0.0).then_inc(consts, 1)
            nc.gpsimd.memset(xnT[:, :, 0:1], 0.0).then_inc(consts, 1)
            for v in v_sb:
                nc.gpsimd.memset(v[:, :, 1, :], 1.0).then_inc(consts, 1)
            pool.wait_ge(c_in, 16 * 8)
            pool.wait_ge(consts, 8)

            def invert(m):
                pool.wait_ge(ln_stats, m + 1)
                nc.gpsimd.tensor_tensor(rstd[:, :], veps[:, :], minus_half[:, :], ALU.pow).then_inc(ln_rstd, 1)

            def batch(b, par):
                attends, front, prev, ahead = flags(b)
                n, npar = b + 1, 1 - par
                for g in range(NG):
                    for s in range(STEPS):
                        here = (g, s)
                        if here == AT["rstd"] and ahead:
                            invert(b + 2)
                        if front:
                            if here == AT["diff"]:
                                pool.wait_ge(xn_hi, DC * (n + 1))
                                pool.wait_ge(y_ready, past(n))
                                nc.gpsimd.tensor_tensor(diff[:, :, :], xnT[:, :, 1:S + 1], xnT[:, :, 0:S],
                                                        ALU.subtract).then_inc(diff_ready, 1)
                            for k, at in enumerate((AT["rope_q_add"], AT["rope_k_add"])):
                                if here == at:
                                    pool.wait_ge(rotated, 2 * n + k + 1)
                                    nc.gpsimd.tensor_tensor(rot[:, 0, :], rot[:, 0, :], tmp[:, 1, :], ALU.subtract)
                                    nc.gpsimd.tensor_tensor(rot[:, 1, :], rot[:, 1, :], tmp[:, 0, :], ALU.add).then_inc(rope_done, 1)
                            for k, (at, parts, loaded) in enumerate(((AT["split_q_lo"], q_parts, q_loaded), (AT["split_k_lo"], k_parts, k_loaded))):
                                if here == at:
                                    pool.wait_ge(qk_hi, 2 * n + k + 1)
                                    for half in range(2):
                                        pool.wait_ge(loaded[half], past((Q_DMAS, K_DMAS)[k] * n))
                                    nc.gpsimd.tensor_tensor(parts[:, 1, :, :], rot[:, :, :], parts[:, 0, :, :].bitcast(F32),
                                                            ALU.subtract).then_inc(qk_lo, 1)
                            for k, at in enumerate((AT["mix_k_lo"], AT["mix_r_lo"])):
                                if here == at:
                                    pool.wait_ge(mix_hi, 2 * n + k + 1)
                                    if k == 1:
                                        pool.wait_ge(unit_full, unit_count(b, "K1"))
                                    elif ran(b - 1):
                                        pool.wait_ge(unit_full, unit_count(b - 1, "R1"))
                                    nc.gpsimd.tensor_tensor(b_lo[:, :, :], mix[:, :, :], b_hi[:, :, :].bitcast(F32),
                                                            ALU.subtract).then_inc(mix_lo, 1)
                            if here == AT["ksq_split_lo"]:
                                pool.wait_ge(ksq_hi, n + 1)
                                pool.wait_ge(unit_full, unit_count(b, "O1" if prev else "K1"))
                                nc.gpsimd.tensor_tensor(a_lo[:, :, :], relu_k[:, :, :], a_hi[:, :, :].bitcast(F32),
                                                        ALU.subtract).then_inc(ksq_lo, 1)
                            if here == AT["sigmoid"]:
                                pool.wait_ge(unit_free, unit_count(b, "R1"))
                                pool.sem_inc(gpsimd_passed, 1)
                                nc.gpsimd.tensor_scalar(act_sb[:, :], act_sb[:, :], 0.5, 0.5, ALU.mult, ALU.add).then_inc(r_ready, 1)
                            if here == AT["y_bias"]:
                                pool.wait_ge(y_loaded, 16 * (n + 1))
                                nc.gpsimd.tensor_tensor(y[npar][:, :, :], y[npar][:, :, :],
                                                        bo_sb[:, :].unsqueeze(1).to_broadcast([P, TT, D]), ALU.add).then_inc(y_biased, 1)
                            if here == AT["y_gate"]:
                                pool.wait_ge(y_biased, n + 1)
                                pool.wait_ge(unit_free, unit_count(b, "F1"))
                                nc.gpsimd.tensor_tensor(y[npar][:, :, :], y[npar][:, :, :], r_sb[:, :, :], ALU.add).then_inc(y_ready, 1)
                        if here == AT["attn_split_lo"] and prev:
                            pool.wait_ge(attn_hi, b)
                            pool.wait_ge(unit_full, unit_count(b, "V1") if front else unit_count(b - 1, "F1"))
                            nc.gpsimd.tensor_tensor(a_lo[:, :, :], tmp[:, :, :], a_hi[:, :, :].bitcast(F32),
                                                    ALU.subtract).then_inc(attn_lo, 1)

            invert(0)
            for stack in (k_stack, q_stack):
                nc.gpsimd.memset(stack[:, :, :].bitcast(F32), 0.0).then_inc(zeroed, 1)
            program(pool, batch)


def kernel(**inputs):
    import numpy as _np
    import concourse.bacc as _bacc
    from concourse import mybir as _mybir
    from concourse.bass_utils import run_bass_kernel_spmd as _run

    def get(name):
        return _np.ascontiguousarray(inputs[name])

    half, pair, head = _np.meshgrid(_np.arange(2), _np.arange(8), _np.arange(8), indexing="ij")
    even = ((half * 8 + head) * DK + 2 * pair).ravel()
    perm = _np.concatenate([even, even + 1])
    q, j, d, par = _np.meshgrid(_np.arange(2), _np.arange(4), _np.arange(DK), _np.arange(2), indexing="ij")
    feature = ((GH * (2 * q + par) + j) * DK + d).reshape(P, 2)

    def by_chunk(w):
        return _np.ascontiguousarray(w.T.reshape(DC, P, D).transpose(1, 0, 2))

    inv_freq = (1.0 / _np.float32(10000.0) ** (_np.arange(0, DK, 2, dtype=_np.float32) / _np.float32(DK))).astype(_np.float32)
    angles = _np.arange(S).astype(_np.float32)[None, :] * inv_freq[pair.ravel()][:, None]
    arrays = {
        "x": get("L0_attn_x"),
        "wq": by_chunk(get("L0_attn_Wq")[perm]), "wk": by_chunk(get("L0_attn_Wk")[perm]), "wv": by_chunk(get("L0_attn_Wv")),
        "wo": _np.ascontiguousarray(get("L0_attn_Wo").T[feature]),
        "wr": by_chunk(get("L0_ffn_W_r")), "wf": by_chunk(get("L0_ffn_W_k")), "wc": by_chunk(get("L0_ffn_W_v")),
        "bq": _np.ascontiguousarray(get("L0_attn_bq")[perm].reshape(2, P).T),
        "bk": _np.ascontiguousarray(get("L0_attn_bk")[perm].reshape(2, P).T),
        "bv": get("L0_attn_bv"), "bo": get("L0_attn_bo"),
        "mu_r": _np.ascontiguousarray(get("L0_ffn_mu_r").reshape(DC, P).T),
        "mu_k": _np.ascontiguousarray(get("L0_ffn_mu_k").reshape(DC, P).T),
        "cos_t": _np.cos(angles).astype(_np.float32), "sin_t": _np.sin(angles).astype(_np.float32),
    }
    nc = _bacc.Bacc("TRN2", target_bir_lowering=False, num_devices=1)
    args = {}
    for name, a in arrays.items():
        args[name] = nc.dram_tensor(f"in_{name}", a.shape, _mybir.dt.from_np(a.dtype), kind="ExternalInput").ap()
    out = nc.dram_tensor("out_x", (B, S, D), _mybir.dt.float32, kind="ExternalOutput").ap()
    layer_kernel(nc, **args, out=out)
    r = _run(nc, [{f"in_{name}": a for name, a in arrays.items()}], core_ids=[0])
    return r.results[0]["out_x"]
```
